# Optimizing a Trainium2 kernel written in Bass

```python
import numpy as np
import jax
import jax.numpy as jnp

def _softmax(x, axis=-1):
    return jax.nn.softmax(x, axis=axis)

def _gelu(x):
    return jax.nn.gelu(x, approximate=True)

def _silu(x):
    return jax.nn.silu(x)

def _sigmoid(x):
    return jax.nn.sigmoid(x)

def _layernorm(x, axis=-1, eps=1e-05):
    m = jnp.mean(x, axis=axis, keepdims=True)
    v = jnp.var(x, axis=axis, keepdims=True)
    return (x - m) / jnp.sqrt(v + eps)

def _scatter_add(tgt, idx, src, axis=0):
    return tgt.at[idx].add(src)

def _segment_sum(src, seg, n):
    return jax.ops.segment_sum(src, seg, n)
kernel_name = 'mk_macaron_d1_jaxref_r8_ea3fe9'

def setup_inputs(seed: int=0):
    np.random.seed(seed)
    _w = jnp.asarray

    def _L0_attn_setup():
        import jax, jax.numpy as jnp
        import numpy as np
        import math
        WINDOW = 64
        N_HEAD = 16
        key = jax.random.key(seed)
        ks = jax.random.split(key, 5)
        B, L, D = (2, 512, 128)
        s = 0.02
        return {'x': jax.random.normal(ks[0], (B, L, D), dtype=jnp.float32), 'Wq': jax.random.normal(ks[1], (D, D), dtype=jnp.float32) * s, 'bq': jnp.zeros((D,), jnp.float32), 'Wk': jax.random.normal(ks[2], (D, D), dtype=jnp.float32) * s, 'bk': jnp.zeros((D,), jnp.float32), 'Wv': jax.random.normal(ks[3], (D, D), dtype=jnp.float32) * s, 'bv': jnp.zeros((D,), jnp.float32), 'Wo': jax.random.normal(ks[4], (D, D), dtype=jnp.float32) * s, 'bo': jnp.zeros((D,), jnp.float32)}
    _L0_attn_in = _L0_attn_setup()

    def _L0_ffn_setup():
        import jax, jax.numpy as jnp
        import numpy as np
        B, L, D = (2, 128, 128)
        HID, E, K = (256, 8, 2)
        key = jax.random.key(seed)
        ks = jax.random.split(key, 4)
        std = 0.02
        return {'x': jax.random.normal(ks[0], (B, L, D), dtype=jnp.float32), 'router_scale': jnp.ones((D,), dtype=jnp.float32), 'router_w': jax.random.normal(ks[1], (D, E), dtype=jnp.float32) * std, 'gating_w': jax.random.normal(ks[2], (E, 2, HID, D), dtype=jnp.float32) * std, 'linear_w': jax.random.normal(ks[3], (E, HID, D), dtype=jnp.float32) * std, 'per_expert_scale': jnp.ones((E,), dtype=jnp.float32)}
    _L0_ffn_in = _L0_ffn_setup()
    _d = {'L0_attn_x': _L0_attn_in['x'], 'L0_attn_Wq': _L0_attn_in['Wq'], 'L0_attn_bq': _L0_attn_in['bq'], 'L0_attn_Wk': _L0_attn_in['Wk'], 'L0_attn_bk': _L0_attn_in['bk'], 'L0_attn_Wv': _L0_attn_in['Wv'], 'L0_attn_bv': _L0_attn_in['bv'], 'L0_attn_Wo': _L0_attn_in['Wo'], 'L0_attn_bo': _L0_attn_in['bo'], 'L0_ffn_router_scale': _L0_ffn_in['router_scale'], 'L0_ffn_router_w': _L0_ffn_in['router_w'], 'L0_ffn_gating_w': _L0_ffn_in['gating_w'], 'L0_ffn_linear_w': _L0_ffn_in['linear_w'], 'L0_ffn_per_expert_scale': _L0_ffn_in['per_expert_scale']}
    _x0 = _d['L0_attn_x']
    _d['L0_attn_x'] = jax.random.normal(jax.random.fold_in(jax.random.key(seed), 1), (16, 256, 128), dtype=_x0.dtype)
    del _x0
    return _d

def reference(L0_attn_x, L0_attn_Wq, L0_attn_bq, L0_attn_Wk, L0_attn_bk, L0_attn_Wv, L0_attn_bv, L0_attn_Wo, L0_attn_bo, L0_ffn_router_scale, L0_ffn_router_w, L0_ffn_gating_w, L0_ffn_linear_w, L0_ffn_per_expert_scale):

    def _L0_attn_ref(x, Wq, bq, Wk, bk, Wv, bv, Wo, bo):
        import jax, jax.numpy as jnp
        import numpy as np
        import math
        WINDOW = 64
        N_HEAD = 16
        B, L, D = x.shape
        W, H = (WINDOW, N_HEAD)
        dh = D // H
        C = L // W
        scale = 1.0 / math.sqrt(dh)
        q = x @ Wq.T + bq
        k = x @ Wk.T + bk
        v = x @ Wv.T + bv
        kp = jnp.pad(k, ((0, 0), (W, 0), (0, 0)))
        vp = jnp.pad(v, ((0, 0), (W, 0), (0, 0)))
        idx = jnp.arange(C)[:, None] * W + jnp.arange(2 * W)[None, :]
        kc = kp[:, idx].reshape(B, C, 2 * W, H, dh)
        vc = vp[:, idx].reshape(B, C, 2 * W, H, dh)
        qc = q.reshape(B, C, W, H, dh)
        scores = jnp.einsum('bcqhd,bckhd->bchqk', qc, kc) * scale
        valid = idx >= W
        scores = jnp.where(valid[None, :, None, None, :], scores, jnp.float32(-1000000000.0))
        attn = jax.nn.softmax(scores, axis=-1)
        out = jnp.einsum('bchqk,bckhd->bcqhd', attn, vc).reshape(B, L, D)
        return out @ Wo.T + bo

    def _L0_ffn_ref(x, router_scale, router_w, gating_w, linear_w, per_expert_scale):
        import jax, jax.numpy as jnp
        import numpy as np
        B, L, D = (2, 128, 128)
        HID, E, K = (256, 8, 2)
        d = x.shape[-1]
        var = jnp.mean(jnp.square(x), axis=-1, keepdims=True)
        r_in = x * jax.lax.rsqrt(var + 1e-06)
        r_in = r_in * jax.lax.rsqrt(jnp.array(d, dtype=r_in.dtype)) * router_scale
        logits = jnp.dot(r_in, router_w).astype(jnp.float32)
        probs = jax.nn.softmax(logits, axis=-1)
        _, top_k_idx = jax.lax.top_k(logits, K)
        indicator = jax.nn.one_hot(top_k_idx, probs.shape[-1], dtype=probs.dtype)
        gate_weights = indicator.sum(axis=-2) * probs
        renorm = jnp.sum(gate_weights, axis=-1, keepdims=True)
        renorm = jnp.where(renorm > 0.0, renorm, 1.0)
        weights = probs / renorm
        top_k_w = jnp.take_along_axis(weights, top_k_idx, axis=-1)
        combine = jnp.einsum('blke,blk->ble', indicator, top_k_w)
        combine = combine * per_expert_scale
        gate0 = jnp.einsum('bld,ehd->bleh', x, gating_w[:, 0])
        gate1 = jnp.einsum('bld,ehd->bleh', x, gating_w[:, 1])
        act = jax.nn.gelu(gate0) * gate1
        out = jnp.einsum('bleh,ehd,ble->bld', act, linear_w, combine)
        return out.astype(x.dtype)
    x = L0_attn_x
    x = x + 0.5 * _L0_ffn_ref(_layernorm(x, axis=-1), L0_ffn_router_scale, L0_ffn_router_w, L0_ffn_gating_w, L0_ffn_linear_w, L0_ffn_per_expert_scale)
    x = x + _L0_attn_ref(_layernorm(x, axis=-1), L0_attn_Wq, L0_attn_bq, L0_attn_Wk, L0_attn_bk, L0_attn_Wv, L0_attn_bv, L0_attn_Wo, L0_attn_bo)
    x = x + 0.5 * _L0_ffn_ref(_layernorm(x, axis=-1), L0_ffn_router_scale, L0_ffn_router_w, L0_ffn_gating_w, L0_ffn_linear_w, L0_ffn_per_expert_scale)
    return x

_drawn_inputs = setup_inputs


def setup_inputs(seed=0):
    import zlib

    import numpy as np

    out = dict(_drawn_inputs(seed))
    spreads = {'L0_attn_bq': (0.0, 0.8),
     'L0_attn_bk': (0.0, 0.8),
     'L0_attn_bv': (0.0, 0.381),
     'L0_attn_bo': (0.0, 0.1),
     'L0_ffn_router_scale': (1.0, 0.6),
     'L0_ffn_per_expert_scale': (1.0, 0.6)}
    factors = {'L0_attn_Wq': 8.0,
     'L0_attn_Wk': 8.0,
     'L0_attn_Wv': 8.0,
     'L0_ffn_router_w': 8.0,
     'L0_ffn_gating_w': 8.0,
     'L0_ffn_linear_w': 8.0}
    for name, (base, spread) in spreads.items():
        noise = np.random.default_rng([zlib.crc32(name.encode()), seed]).standard_normal(out[name].shape)
        drawn = base * np.exp(spread * noise) if base else spread * noise
        out[name] = jnp.asarray(drawn.astype(out[name].dtype))
    for name, factor in factors.items():
        out[name] = (out[name] * factor).astype(out[name].dtype)
    return out
```

```python
from contextlib import ExitStack

import concourse.bass as bass
from concourse import mybir

F32 = mybir.dt.float32
I32 = mybir.dt.int32
U32 = mybir.dt.uint32
ALU = mybir.AluOpType
ACT = mybir.ActivationFunctionType
AX_X = mybir.AxisListType.X

P = 128
NSEQ, L, D = 16, 256, 128
T = NSEQ * L // P
TG = 4
GROUPS = T // TG
H, DH, W = 16, 8, 64
NP = H // 2
C = L // W
UNITS = TG * P // W
VW = 2 * DH + 1
PADL = W + L
E, HID, TOPK = 8, 256, 2
GW = 2 * HID
EW = GW + 2 * D
REGION = NSEQ * L + P
SLOTS = 72
SPARE = SLOTS - NSEQ * L * TOPK // P + 1
ROWS = E * REGION + SPARE * P
RING = 4
XRING = 2 * RING
CLAMPED = "computed on chip from counts that add up to the tokens, and clamped"
SCALE = float(DH) ** -0.5
LN_EPS, RMS_EPS = 1e-5, 1e-6
LOW = -3.0e38


def need(eng, sem, value):
    if not (isinstance(value, int) and value <= 0):
        eng.wait_ge(sem, value)


class Steps:

    def __init__(self, eng, sem):
        self.eng, self.sem, self.base, self.n = eng, sem, 0, 0

    def __call__(self, ins):
        self.n += 1
        ins.then_inc(self.sem, 1)
        self.eng.wait_ge(self.sem, self.base + self.n)

    def later(self, ins):
        self.n += 1
        ins.then_inc(self.sem, 1)

    def wait(self):
        self.eng.wait_ge(self.sem, self.base + self.n)

    def enter(self, index, first, per):
        self.outside = self.base + self.n
        self.base, self.n, self.per = self.outside + (index - first) * per, 0, per

    def leave(self, times):
        assert self.n == self.per, f"steps in the body: {self.n}, not {self.per}"
        self.base, self.n = self.outside + times * self.per, 0


def macaron(nc, x, wq, bq, wk, bk, wv, bv, wo, bo, rscale, rw, experts, pes, consts, out):
    xs = nc.dram_tensor("xs_rows", [ROWS, D], F32, kind="Internal").ap()
    ys = nc.dram_tensor("ys_rows", [SLOTS * P, D], F32, kind="Internal").ap()
    x_tiles = x.rearrange("(t p) d -> p t d", p=P)
    out_tiles = out.rearrange("(t p) d -> p t d", p=P)
    ys_tiles = ys.rearrange("(s p) d -> p s d", p=P)

    with ExitStack() as ctx:
        def sb(name, shape, dt=F32):
            return ctx.enter_context(nc.sbuf_tensor(name, shape, dt))

        def sem(name):
            return ctx.enter_context(nc.semaphore(name))

        X = sb("X", [P, T, D])
        EXP = sb("EXP", [P, E * EW])
        WQ, WK, WV = sb("WQ", [P, D]), sb("WK", [P, D]), sb("WV", [P, D])
        WO = sb("WO", [P, D])
        BQ, BK = sb("BQ", [P, 1]), sb("BK", [P, 1])
        BQS = sb("BQS", [P, 1])
        BV, BO = sb("BV", [P, D]), sb("BO", [P, D])
        RS, RW, RWS = sb("RS", [P, 1]), sb("RW", [P, E]), sb("RWS", [P, E])
        PES = sb("PES", [P, E])
        CN = sb("CN", [P, consts.shape[1]])
        o = 0
        parts = []
        for n in (P, P, P, H, E, E, E * (TG * GROUPS + 1), SLOTS * E, E * E, SLOTS):
            parts.append(CN[:, o:o + n])
            o += n
        IDN, BEFORE, ONES, HMASK, DESC, REG0, KTH, SIOTA, TRI, SROW = parts
        QT = sb("QT", [P, GROUPS, TG * P])
        KT = sb("KT", [P, NSEQ, PADL])
        V = sb("V", [P, GROUPS * UNITS, NP, VW])
        POSI = sb("POSI", [P, T + TG, TOPK], U32)
        CW = sb("CW", [P, T, TOPK])
        NHALF, REPS, EULER = sb("NHALF", [P, T]), sb("REPS", [P, T]), sb("EULER", [P, TG])
        ZROW = sb("ZROW", [P, SPARE, D])
        ALL, LN, RT = [{m: sb(f"{m}_{which}", [P, n]) for m in ("mean", "var", "vareps", "rstd", "msq", "stok")}
                       for which, n in (("all", T), ("ln", TG), ("rt", TG))]
        BST = sb("BST", [P, T, 6])
        MSUM, MDIF, M2S = sb("MSUM", [P, T]), sb("MDIF", [P, T]), sb("M2S", [P, T])
        XN = [sb(f"XN{i}", [P, TG, D]) for i in range(2)]
        XNT = sb("XNT", [P, TG * P])
        LGS, L2 = sb("LGS", [P, TG, E]), sb("L2", [P, TG, E])
        M12 = sb("M12", [P, TOPK, TG])
        EQ, KM = sb("EQ", [P, TG, E]), sb("KM", [P, TG])
        OH = sb("OH", [P, TOPK, T, E])
        IND = sb("IND", [P, TG, E])
        DL, EX, WZ = sb("DL", [P, TG]), sb("EX", [P, TG]), sb("WZ", [P, TG])
        OHP, PK = sb("OHP", [P, TOPK, TG, E]), sb("PK", [P, TOPK, TG])
        BT = sb("BT", [P, TG + 1, E])
        POSM = sb("POSM", [P, TG, E])
        ROWF = sb("ROWF", [P, TOPK, T])
        OHD, YOFF = sb("OHD", [P, TOPK * T, E]), sb("YOFF", [P, TOPK * T])
        IDX = [sb(f"IDX{i}", [P, TOPK, TG], U32) for i in range(2)]
        GIDX = sb("GIDX", [P, TG, TOPK], U32)
        YG = sb("YG", [P, TG, TOPK, D])
        CNT, NT, END = sb("CNT", [P, E]), sb("NT", [P, E]), sb("END", [P, E])
        CMP = sb("CMP", [P, E * (TG * GROUPS + 1)])
        SLT = sb("SLT", [P, SLOTS * E])
        EID, ST0 = sb("EID", [P, SLOTS]), sb("ST0", [P, SLOTS])
        ROWI, WOFI, TAILI = sb("ROWI", [P, SLOTS], I32), sb("WOFI", [P, SLOTS], I32), sb("TAILI", [P, E], I32)
        XS = sb("XS", [P, XRING, D])
        XST = [sb(f"XST{i}", [P, P]) for i in range(2)]
        GA = [sb(f"GA{i}", [P, HID]) for i in range(2)]
        AV = [sb(f"AV{i}", [P, HID]) for i in range(2)]
        AVT = [sb(f"AVT{i}", [P, HID]) for i in range(2)]
        YO = [sb(f"YO{i}", [P, RING, D]) for i in range(2)]
        XA = sb("XA", [P, TG, D])
        XAT = sb("XAT", [P, 2, PADL])
        QM = [sb(f"QM{i}", [P, NP, 2, W]) for i in range(2)]
        MX = [sb(f"MX{i}", [P, NP]) for i in range(2)]
        PR = [sb(f"PR{i}", [P, NP, 2 * W]) for i in range(C)]
        PT = [sb(f"PT{i}", [P, NP, P]) for i in range(2)]
        RD = sb("RD", [P, NP])
        OS = sb("OS", [P, 2, NP, DH])
        OT = sb("OT", [P, 2, 2, W])

        PS = ctx.enter_context(nc.psum_tensor("PS", [P, 8, 512], F32))
        HPS = [PS[:, i, :] for i in range(2)]
        XTP = [PS[:, 2 + i, 0:P] for i in range(2)]
        ATP = [PS[:, 4 + i, 0:HID] for i in range(2)]
        YPS = [PS[:, 6 + i, 0:D] for i in range(2)]
        SPS = [PS[:, 2 * i:2 * i + 2, :].rearrange("p a (b k) -> p (a b) k", k=P) for i in range(2)]
        TPS = PS[:, 4:6, :].rearrange("p a (b k) -> p (a b) k", k=P)
        M0, M1 = PS[:, 6, :], PS[:, 7, :]

        x_loaded = [sem(f"x_loaded{g}") for g in range(2)]
        w_loaded, e_loaded, xs_zeroed = sem("w_loaded"), sem("e_loaded"), sem("xs_zeroed")
        consts_set = sem("consts_set")
        pool_consts = sem("pool_consts")
        dve_step, act_step, pool_step = sem("dve_step"), sem("act_step"), sem("pool_step")
        var_ready, rstd_ready, stok_ready = sem("var_ready"), sem("rstd_ready"), sem("stok_ready")
        diff_ready, exp_ready = sem("diff_ready"), sem("exp_ready")
        xn_ready, rt_done, xnt_ready = sem("xn_ready"), sem("rt_done"), sem("xnt_ready")
        lg_done, ind_ready, px_done = sem("lg_done"), sem("ind_ready"), sem("px_done")
        lg_used, px_used = sem("lg_used"), sem("px_used")
        idx_ready = sem("idx_ready")
        scattered = [sem(f"scattered{i}") for i in range(2)]
        table_ready, tails_zeroed = sem("table_ready"), sem("tails_zeroed")
        xs_in = [sem(f"xs_in{i}") for i in range(XRING)]
        ys_out = [sem(f"ys_out{i}") for i in range(2)]
        xt_done, xst_ready, h_done = sem("xt_done"), sem("xst_ready"), sem("h_done")
        gelu_done, av_ready, at_done = sem("gelu_done"), sem("av_ready"), sem("at_done")
        avt_ready, y_done, yo_ready = sem("avt_ready"), sem("y_done"), sem("yo_ready")
        gidx_ready, gathered, yg_used = sem("gidx_ready"), sem("gathered"), sem("yg_used")
        lnvar_ready, lnrstd_ready = sem("lnvar_ready"), sem("lnrstd_ready")
        xa_ready, xat_done, xat_ready = sem("xa_ready"), sem("xat_done"), sem("xat_ready")
        q_done, q_ready, k_done, k_ready = sem("q_done"), sem("q_ready"), sem("k_done"), sem("k_ready")
        v_done, v_ready = sem("v_done"), sem("v_ready")
        qm_ready, s_done, d_ready, p_ready = sem("qm_ready"), sem("s_done"), sem("d_ready"), sem("p_ready")
        t_done, pt_ready, pv_done, o_ready = sem("t_done"), sem("pt_ready"), sem("pv_done"), sem("o_ready")
        ot_done, ot_ready, pj_done, res_done = sem("ot_done"), sem("ot_ready"), sem("pj_done"), sem("res_done")
        posi_ready, stored = sem("posi_ready"), sem("stored")

        WEIGHT_LOADS = 12

        def tiles(g, n=TG):
            return bass.ds(g * TG, n)

        def on(g):
            return not isinstance(g, int) or 0 <= g < GROUPS

        block = ctx.enter_context(nc.Block())

        @block.sync
        def _(sp):
            for h in range(2):
                sp.dma_start(X[:, h * 16:h * 16 + 16, :], x_tiles[:, h * 16:h * 16 + 16, :]).then_inc(x_loaded[h], 16)
            for dst, src in ((CN, consts), (RS, rscale), (RW, rw), (PES, pes), (WQ, wq), (WK, wk), (WV, wv),
                             (BQ, bq), (BK, bk), (BV, bv), (BO, bo)):
                sp.dma_start(dst[:, :], src).then_inc(w_loaded, 16)
            sp.dma_start(WO[:, :], wo).then_inc(w_loaded, 16)
            sp.dma_start(EXP[:, :], experts).then_inc(e_loaded, 16)
            sp.wait_ge(pool_consts, 1)
            sp.dma_start(xs[E * REGION:ROWS, :].rearrange("(n p) d -> p n d", p=P), ZROW[:, :, :]).then_inc(xs_zeroed, 16)

            def row_at(reg, entry, high):
                sp.load(reg, entry)
                return nc.s_assert_within(sp.snap(reg), min_val=0, max_val=high, skip_runtime_bounds_check_because=CLAMPED)

            row_regs = [sp.alloc_register(f"row{r}") for r in range(XRING)]

            def ffn(ph):
                sp.wait_ge(table_ready, ph + 1)
                for e in range(E):
                    r = row_at(row_regs[e], TAILI[0:1, e:e + 1], ROWS - P)
                    sp.dma_start(xs[bass.ds(r, P), :], ZROW[:, 0, :]).then_inc(tails_zeroed, 16)
                sp.wait_ge(tails_zeroed, 16 * E * (ph + 1))
                sp.wait_ge(xs_zeroed, 16)
                sp.wait_ge(scattered[0], 16 * TG * TOPK * (GROUPS // 2 + GROUPS * ph))
                sp.wait_ge(scattered[1], 16 * TG * TOPK * (GROUPS // 2))
                b = SLOTS * ph

                def load(s, r):
                    need(sp, xt_done, b + s - XRING + 1)
                    row = row_at(row_regs[r], ROWI[0:1, bass.ds(s, 1)], ROWS - P)
                    sp.dma_start(XS[:, r, :], xs[bass.ds(row, P), :]).then_inc(xs_in[r], 16)

                def store(i, par):
                    sp.wait_ge(yo_ready, b + (i + 1) * RING)
                    sp.dma_start(ys_tiles[:, bass.ds(i * RING, RING), :], YO[par][:, :, :]).then_inc(ys_out[par], 16)

                for s in range(XRING):
                    load(s, s)
                with sp.Fori(0, SLOTS // XRING - 1) as i:
                    for par in range(2):
                        store(i * 2 + par, par)
                        for r in range(par * RING, (par + 1) * RING):
                            load(i * XRING + XRING + r, r)
                for par in range(2):
                    store(SLOTS // RING - 2 + par, par)

            ffn(0)
            ffn(1)
            with sp.Fori(0, GROUPS) as g:
                sp.wait_ge(yg_used, GROUPS + g + 1)
                sp.dma_start(out_tiles[:, tiles(g), :], X[:, tiles(g), :]).then_inc(stored, 16)
            sp.wait_ge(stored, 16 * GROUPS)

        @block.gpsimd
        def _(pool):
            pool.memset(ZROW[:, :, :], 0.0).then_inc(pool_consts, 1)
            step = Steps(pool, pool_step)
            step.later(pool.memset(NHALF[:, :], -0.5))
            step.later(pool.memset(REPS[:, :], RMS_EPS))
            step(pool.memset(EULER[:, :], 2.718281828459045))

            def router_scales(st, n, done):
                rstd, msq, stok = st["rstd"][:, :], st["msq"][:, :], st["stok"][:, :]
                pool.tensor_tensor(rstd, st["vareps"][:, :], NHALF[:, 0:n], ALU.pow).then_inc(rstd_ready, 1)
                pool.wait_ge(rstd_ready, done + 1)
                step(pool.tensor_tensor(msq, rstd, rstd, ALU.mult))
                step(pool.tensor_tensor(msq, msq, st["var"][:, :], ALU.mult))
                step(pool.tensor_tensor(msq, msq, REPS[:, 0:n], ALU.add))
                pool.tensor_tensor(stok, msq, NHALF[:, 0:n], ALU.pow).then_inc(stok_ready, 1)

            def route(k, par):
                pool.wait_ge(diff_ready, k + 1)
                pool.wait_ge(idx_ready, k + 1)
                pool.wait_ge(xn_ready, TG * (k + 1))
                pool.tensor_tensor(EX[:, :], EULER[:, :], DL[:, :], ALU.pow).then_inc(exp_ready, 1)
                for i in range(TG):
                    for c in range(TOPK):
                        pool.indirect_dma_start(xs, bass.IndirectOffsetOnAxis(ap=IDX[par][:, c, i:i + 1], axis=0),
                                                XN[par][:, i, :], None).then_inc(scattered[par], 16)

            def gather(idx):
                for i in range(TG):
                    for c in range(TOPK):
                        pool.indirect_dma_start(YG[:, i, c, :], None, ys,
                                                bass.IndirectOffsetOnAxis(ap=idx[:, i, c:c + 1], axis=0))\
                            .then_inc(gathered, 16)

            def all_out(ph):
                for par in range(2):
                    pool.wait_ge(ys_out[par], 16 * (SLOTS // XRING) * (ph + 1))

            pool.wait_ge(var_ready, 1)
            router_scales(ALL, T, 0)
            with pool.Fori(0, GROUPS // 2) as i:
                for par in range(2):
                    route(i * 2 + par, par)

            pool.wait_ge(posi_ready, 1)
            all_out(0)
            gather(POSI[:, 0:TG, :])

            def body(g):
                if on(g + 1):
                    pool.wait_ge(lnvar_ready, g + 2)
                    pool.wait_ge(yg_used, g + 2)
                    pool.wait_ge(gathered, 16 * TG * TOPK * (g + 2))
                    pool.tensor_tensor(LN["rstd"][:, :], LN["vareps"][:, :], NHALF[:, 0:TG], ALU.pow)\
                        .then_inc(lnrstd_ready, 1)
                    pool.tensor_copy(GIDX[:, :, :], POSI[:, tiles(g + 2), :]).then_inc(gidx_ready, 1)
                    pool.wait_ge(gidx_ready, g + 2)
                if on(g - 1):
                    pool.wait_ge(var_ready, g + 1)
                    router_scales(RT, TG, g)
                if on(g + 1):
                    gather(GIDX)
                if on(g - 1):
                    route(GROUPS + g - 1, 0)

            body(-1)
            body(0)
            with pool.Fori(1, GROUPS - 1) as g:
                step.enter(g, 1, 3)
                body(g)
                step.leave(GROUPS - 2)
            body(GROUPS - 1)
            body(GROUPS)
            pool.wait_ge(posi_ready, 2)
            all_out(1)
            for g in range(GROUPS):
                pool.wait_ge(yg_used, GROUPS + g)
                gather(POSI[:, g * TG:(g + 1) * TG, :])

        @block.tensor
        def _(pe):
            offsets = [pe.alloc_register(f"weight_offset{r}") for r in range(RING)]

            def transposes_of_router(k, par):
                need(pe, px_used, k)
                pe.wait_ge(xn_ready, TG * (k + 1))
                for i in range(TG):
                    ins = pe.transpose(M1[:, i * P:(i + 1) * P], XN[par][:, i, :], IDN)
                ins.then_inc(rt_done, 1)

            def logits(k):
                pe.wait_ge(xnt_ready, k + 1)
                for i in range(TG):
                    ins = pe.matmul(M1[:, i * E:(i + 1) * E], XNT[:, i * P:(i + 1) * P], RWS[:, :],
                                    start=True, stop=True)
                ins.then_inc(lg_done, 1)

            def prefixes(k):
                pe.wait_ge(ind_ready, k + 1)
                ind = IND[:, :, :].rearrange("p t e -> p (t e)")
                pe.matmul(M1[:, 0:TG * E], BEFORE, ind, start=True, stop=True)
                pe.matmul(M1[:, TG * E:2 * TG * E], ONES, ind, start=True, stop=True).then_inc(px_done, 1)

            def ffn(ph):
                b = SLOTS * ph
                pe.wait_ge(table_ready, ph + 1)

                def transpose_in(s, r, rounds):
                    pe.wait_ge(xs_in[r], 16 * (rounds + 1 + SLOTS // XRING * ph))
                    need(pe, xst_ready, b + s - 1)
                    pe.transpose(XTP[r % 2], XS[:, r, :], IDN).then_inc(xt_done, 1)

                def load_offset(s, r):
                    pe.load(offsets[r % RING], WOFI[0:1, bass.ds(s, 1)])

                def offset(r):
                    return nc.s_assert_within(pe.snap(offsets[r % RING]), min_val=0, max_val=(E - 1) * EW,
                                              skip_runtime_bounds_check_because=CLAMPED)

                def gates(s, r):
                    pe.wait_ge(xst_ready, b + s + 1)
                    need(pe, av_ready, b + s - 1)
                    pe.matmul(HPS[r % 2], XST[r % 2][:, :], EXP[:, bass.ds(offset(r), GW)], start=True, stop=True)\
                        .then_inc(h_done, 1)

                def down(s, r):
                    pe.wait_ge(avt_ready, b + s + 1)
                    need(pe, yo_ready, b + s - 1)
                    o = offset(r)
                    for c in range(2):
                        ins = pe.matmul(YPS[r % 2], AVT[r % 2][:, c * P:(c + 1) * P],
                                        EXP[:, bass.ds(o + (GW + c * D), D)], start=(c == 0), stop=(c == 1))
                    ins.then_inc(y_done, 1)

                def transpose_hidden(s, r):
                    pe.wait_ge(av_ready, b + s + 1)
                    need(pe, avt_ready, b + s - 1)
                    for c in range(2):
                        ins = pe.transpose(ATP[r % 2][:, c * P:(c + 1) * P], AV[r % 2][:, c * P:(c + 1) * P], IDN)
                    ins.then_inc(at_done, 1)

                def step(s, r, i):
                    fixed = isinstance(s, int)
                    if not (fixed and s >= SLOTS - 1):
                        transpose_in(s + 1, (r + 1) % XRING, i + (r + 1) // XRING)
                    if not (fixed and s >= SLOTS):
                        gates(s, r)
                    if not (fixed and s >= SLOTS - 1):
                        load_offset(s + 1, r + 1)
                    if not (fixed and s < 2):
                        down(s - 2, (r - 2) % XRING)
                    if not (fixed and (s < 1 or s > SLOTS)):
                        transpose_hidden(s - 1, (r - 1) % XRING)

                load_offset(0, 0)
                transpose_in(0, 0, 0)
                for s in range(XRING):
                    step(s, s, 0)
                with pe.Fori(1, SLOTS // XRING - 1) as i:
                    for r in range(XRING):
                        step(i * XRING + r, r, i)
                for s in range(SLOTS - XRING, SLOTS + 2):
                    step(s, s % XRING, s // XRING)

            def attend_slot_a(g, j):
                if on(g + 1):
                    if j == 2:
                        pe.wait_ge(xa_ready, g + 2)
                        pe.wait_ge(px_used, GROUPS + g - 1 + 0 if not isinstance(g, int) else max(GROUPS + g - 1, GROUPS))
                        for i in range(TG):
                            ins = pe.transpose(M1[:, i * P:(i + 1) * P], XA[:, i, :], IDN)
                        ins.then_inc(xat_done, 1)
                    if j == 3:
                        pe.wait_ge(xat_ready, g + 2)
                        pe.matmul(M1, WQ[:, :], XAT[:, :, W:PADL], start=True, stop=True).then_inc(q_done, 1)
                    if j == 4:
                        pe.wait_ge(k_ready, g + 2)
                        values(0)
                if on(g - 1):
                    if j == 6:
                        logits(GROUPS + g - 1)
                    if j == 7:
                        prefixes(GROUPS + g - 1)

            def values(half):
                for c in range(C):
                    ins = pe.matmul(M1[:, c * P:(c + 1) * P], XAT[:, half, c * W:c * W + 2 * W], WV[:, :],
                                    start=True, stop=True)
                ins.then_inc(v_done, 1)

            def attend_slot_b(g, j):
                if on(g + 1):
                    if j == 3:
                        pe.wait_ge(q_ready, g + 2)
                        pe.matmul(M1, WK[:, :], XAT[:, :, W:PADL], start=True, stop=True).then_inc(k_done, 1)
                    if j == 4:
                        pe.wait_ge(v_ready, 2 * g + 3)
                        values(1)
                if on(g - 1):
                    if j == 5:
                        if on(g + 1):
                            pe.wait_ge(v_ready, 2 * g + 4)
                        transposes_of_router(GROUPS + g - 1, 0)

            def attend(g, j):
                k = g * UNITS + j

                def of(lag):
                    return not isinstance(k, int) or 0 <= k - lag < GROUPS * UNITS

                attend_slot_a(g, j)
                if of(4):
                    pe.wait_ge(o_ready, 2 * (k - 3))
                    pe.transpose(M0[:, 0:P], OS[:, :, :, :].rearrange("p h a d -> p (h a d)"), IDN).then_inc(ot_done, 1)
                if of(0):
                    if j % C == 0:
                        pe.wait_ge(k_ready, g + 1)
                    pe.wait_ge(qm_ready, k + 1)
                    need(pe, d_ready, k - 1)
                    for p in range(NP):
                        ins = pe.matmul(SPS[j % 2][:, p, :], QM[j % 2][:, p, :, :],
                                        KT[:, g * 2 + j // C, (j % C) * W:(j % C) * W + 2 * W], start=True, stop=True)
                    ins.then_inc(s_done, 1)
                if of(4) and j % 2 == 1:
                    pe.wait_ge(ot_ready, k - 3)
                    for h in range(2):
                        ins = pe.matmul(M0[:, 0:D], OT[:, h, :, :], WO[:, :], start=(h == 0), stop=(h == 1))
                    ins.then_inc(pj_done, 1)
                if of(2):
                    pe.wait_ge(p_ready, k - 1)
                    need(pe, pt_ready, k - 2)
                    for p in range(NP):
                        ins = pe.transpose(TPS[:, p, :], PR[(j - 2) % C][:, p, :], IDN)
                    ins.then_inc(t_done, 1)
                attend_slot_b(g, j)
                if of(3):
                    pe.wait_ge(pt_ready, k - 2)
                    pe.wait_ge(v_ready, half_of(g, j))
                    if of(4):
                        if j % 2 == 1:
                            pe.wait_ge(res_done, tile_of(g, j))
                        else:
                            pe.wait_ge(ot_ready, k - 3)
                    for p in range(NP):
                        ins = pe.matmul(M0[:, p * VW:(p + 1) * VW], PT[(j - 3) % 2][:, p, :],
                                        V[:, k - 3, p, :], start=True, stop=True)
                    ins.then_inc(pv_done, 1)

            def half_of(g, j):
                return g * 2 + ((j - 3) // C) + 1

            def tile_of(g, j):
                return g * TG + (j - 5) // 2 + 1

            pe.wait_ge(w_loaded, 16 * WEIGHT_LOADS)
            pe.wait_ge(consts_set, 1)
            with pe.Fori(0, GROUPS // 2) as i:
                for par in range(2):
                    transposes_of_router(i * 2 + par, par)
                    logits(i * 2 + par)
                    prefixes(i * 2 + par)
            need(pe, px_used, GROUPS)
            pe.wait_ge(e_loaded, 16)
            ffn(0)
            pe.wait_ge(avt_ready, SLOTS)
            pe.wait_ge(yo_ready, SLOTS)
            for j in range(UNITS):
                attend_slot_a(-1, j)
                attend_slot_b(-1, j)
            for j in range(UNITS):
                attend(0, j)
            with pe.Fori(1, GROUPS - 1) as g:
                for j in range(UNITS):
                    attend(g, j)
            for g in range(GROUPS - 1, GROUPS + 1):
                for j in range(UNITS):
                    attend(g, j)
            pe.wait_ge(px_used, 2 * GROUPS)
            ffn(1)

        @block.scalar
        def _(act):
            def router_rows(k):
                act.wait_ge(rt_done, k + 1)
                need(act, lg_done, k)
                act.copy(XNT[:, :], M1).then_inc(xnt_ready, 1)

            def ffn(ph):
                b = SLOTS * ph

                def rows(s, r):
                    act.wait_ge(xt_done, b + s + 1)
                    need(act, h_done, b + s - 1)
                    act.copy(XST[r % 2][:, :], XTP[r % 2]).then_inc(xst_ready, 1)

                def gelu(s, r):
                    act.wait_ge(h_done, b + s + 1)
                    need(act, av_ready, b + s - 1)
                    act.activation(GA[r % 2][:, :], HPS[r % 2][:, 0:HID], ACT.Gelu_apprx_tanh).then_inc(gelu_done, 1)

                def acts(s, r):
                    act.wait_ge(at_done, b + s + 1)
                    need(act, y_done, b + s - 1)
                    act.copy(AVT[r % 2][:, :], ATP[r % 2]).then_inc(avt_ready, 1)

                def step(s, r):
                    fixed = isinstance(s, int)
                    if not (fixed and s > SLOTS - 2):
                        rows(s + 1, (r + 1) % RING)
                    if not (fixed and s >= SLOTS):
                        gelu(s, r)
                    if not (fixed and s < 1):
                        acts(s - 1, (r - 1) % RING)

                rows(0, 0)
                for s in range(RING):
                    step(s, s)
                with act.Fori(1, SLOTS // RING - 1) as i:
                    for r in range(RING):
                        step(i * RING + r, r)
                for s in range(SLOTS - RING, SLOTS + 1):
                    step(s, s % RING)

            def prep(g, j):
                if on(g) and j == 2:
                    act.wait_ge(xat_done, g + 1)
                    need(act, v_done, 2 * g)
                    act.copy(XAT[:, :, W:PADL], M1.rearrange("p (s t) -> p s t", s=2)).then_inc(xat_ready, 1)
                if on(g) and j == 3:
                    act.wait_ge(q_done, g + 1)
                    act.activation(QT[:, g, :], M1, ACT.Identity, bias=BQS[:, :], scale=SCALE).then_inc(q_ready, 1)
                    act.wait_ge(k_done, g + 1)
                    act.activation(KT[:, bass.ds(g * 2, 2), W:PADL], M1.rearrange("p (s t) -> p s t", s=2),
                                   ACT.Identity, bias=BK[:, :]).then_inc(k_ready, 1)

            def attend(g, j):
                k = g * UNITS + j

                def of(lag):
                    return not isinstance(k, int) or 0 <= k - lag < GROUPS * UNITS

                if of(1):
                    c = (j - 1) % C
                    act.wait_ge(d_ready, k)
                    pr = PR[c][:, :, W:] if c == 0 else PR[c][:, :, :]
                    act.activation(pr, pr, ACT.Exp).then_inc(p_ready, 1)
                if of(4):
                    act.wait_ge(ot_done, k - 3)
                    if (j - 4) % 2 == 0:
                        need(act, pj_done, pairs_before(g, j))
                    act.copy(OT[:, :, (j - 4) % 2, :], M0[:, 0:P].rearrange("p (h q) -> p h q", h=2))\
                        .then_inc(ot_ready, 1)
                if of(2):
                    act.wait_ge(t_done, k - 1)
                    need(act, pv_done, k - 3)
                    act.copy(PT[(j - 2) % 2][:, :, :], TPS).then_inc(pt_ready, 1)
                prep(g + 1, j)
                if on(g - 1) and j == 5:
                    router_rows(GROUPS + g - 1)

            def pairs_before(g, j):
                return g * TG + (j - 4) // 2

            act.wait_ge(w_loaded, 16 * WEIGHT_LOADS)
            act.mul(BQS[:, :], BQ[:, :], SCALE).then_inc(act_step, 1)
            act.wait_ge(act_step, 1)
            with act.Fori(0, GROUPS) as g:
                router_rows(g)
            ffn(0)
            for j in range(UNITS):
                prep(0, j)
            for j in range(UNITS):
                attend(0, j)
            with act.Fori(1, GROUPS - 1) as g:
                for j in range(UNITS):
                    attend(g, j)
            for g in range(GROUPS - 1, GROUPS + 1):
                for j in range(UNITS):
                    attend(g, j)
            ffn(1)

        @block.vector
        def _(dve):
            step = Steps(dve, dve_step)

            def row_stats(g, bst):
                for i in range(TG):
                    step.later(dve.bn_stats(bst[:, i, :], X[:, g * TG + i, :]))

            def moments(st, n):
                m0, q0, m1, q1 = (BST[:, 0:n, i] for i in (1, 2, 4, 5))
                step.wait()
                step.later(dve.tensor_tensor(MSUM[:, 0:n], m0, m1, ALU.add))
                step.later(dve.tensor_tensor(MDIF[:, 0:n], m0, m1, ALU.subtract))
                step(dve.tensor_tensor(M2S[:, 0:n], q0, q1, ALU.add))
                step.later(dve.tensor_scalar(st["mean"][:, :], MSUM[:, 0:n], 0.5, None, ALU.mult))
                step(dve.scalar_tensor_tensor(out=MDIF[:, 0:n], in0=MDIF[:, 0:n], scalar=0.25, in1=MDIF[:, 0:n],
                                              op0=ALU.mult, op1=ALU.mult))
                step(dve.scalar_tensor_tensor(out=st["var"][:, :], in0=M2S[:, 0:n], scalar=1.0 / D, in1=MDIF[:, 0:n],
                                              op0=ALU.mult, op1=ALU.add))
                return dve.tensor_scalar(st["vareps"][:, :], st["var"][:, :], LN_EPS, None, ALU.add)

            def normalise(dst, t, i, st, a):
                return dve.tensor_scalar(dst[:, i, :], X[:, t, :], st["mean"][:, a], st["rstd"][:, a],
                                         ALU.subtract, ALU.mult)

            def one_hot(logits, c, g):
                step(dve.tensor_reduce(M12[:, c, :], logits, AX_X, ALU.max))
                step(dve.tensor_tensor(EQ[:, :, :], logits, M12[:, c, :].unsqueeze(2).broadcast_to([P, TG, E]), ALU.is_equal))
                step(dve.tensor_tensor(EQ[:, :, :], EQ[:, :, :], DESC.unsqueeze(1).broadcast_to([P, TG, E]), ALU.mult))
                step(dve.tensor_reduce(KM[:, :], EQ[:, :, :], AX_X, ALU.max))
                step(dve.tensor_tensor(OH[:, c, tiles(g), :], EQ[:, :, :], KM[:, :].unsqueeze(2).broadcast_to([P, TG, E]), ALU.is_equal))

            def choose(k, g, stok):
                dve.wait_ge(lg_done, k + 1)
                dve.tensor_tensor(LGS[:, :, :], M1[:, 0:TG * E].rearrange("p (t e) -> p t e", e=E),
                                  stok.unsqueeze(2).broadcast_to([P, TG, E]), ALU.mult).then_inc(lg_used, 1)
                dve.wait_ge(lg_used, k + 1)
                one_hot(LGS[:, :, :], 0, g)
                step(dve.scalar_tensor_tensor(out=L2[:, :, :], in0=OH[:, 0, tiles(g), :], scalar=LOW, in1=LGS[:, :, :],
                                              op0=ALU.mult, op1=ALU.add))
                one_hot(L2[:, :, :], 1, g)
                dve.tensor_tensor(IND[:, :, :], OH[:, 0, tiles(g), :], OH[:, 1, tiles(g), :], ALU.add).then_inc(ind_ready, 1)
                dve.tensor_tensor(DL[:, :], M12[:, 1, :], M12[:, 0, :], ALU.subtract).then_inc(diff_ready, 1)

            def place(k, g, par):
                dve.wait_ge(px_done, k + 1)
                for i in range(TG):
                    step(dve.tensor_tensor(BT[:, i + 1, :], M1[:, (TG + i) * E:(TG + i + 1) * E], BT[:, i, :], ALU.add))
                dve.tensor_tensor(POSM[:, :, :], M1[:, 0:TG * E].rearrange("p (t e) -> p t e", e=E), BT[:, 0:TG, :],
                                  ALU.add).then_inc(px_used, 1)
                dve.wait_ge(px_used, k + 1)
                step(dve.tensor_copy(BT[:, 0, :], BT[:, TG, :]))
                for c in range(TOPK):
                    ins = dve.tensor_tensor(OHP[:, c, :, :], OH[:, c, tiles(g), :], POSM[:, :, :], ALU.mult)
                    step(ins)
                step(dve.tensor_reduce(ROWF[:, :, tiles(g)], OHP[:, :, :, :], AX_X, ALU.add))
                dve.tensor_scalar(IDX[par][:, :, :], ROWF[:, :, tiles(g)], 0.0, None, ALU.add).then_inc(idx_ready, 1)
                for c in range(TOPK):
                    step(dve.tensor_tensor(OHP[:, c, :, :], OH[:, c, tiles(g), :], PES[:, :].unsqueeze(1).broadcast_to([P, TG, E]),
                                           ALU.mult))
                step(dve.tensor_reduce(PK[:, :, :], OHP[:, :, :, :], AX_X, ALU.add))
                dve.wait_ge(exp_ready, k + 1)
                step(dve.tensor_scalar(WZ[:, :], EX[:, :], 1.0, None, ALU.add))
                step(dve.reciprocal(WZ[:, :], WZ[:, :]))
                step.later(dve.scalar_tensor_tensor(out=CW[:, tiles(g), 0], in0=PK[:, 0, :], scalar=0.5, in1=WZ[:, :],
                                              op0=ALU.mult, op1=ALU.mult))
                step(dve.tensor_tensor(WZ[:, :], WZ[:, :], EX[:, :], ALU.mult))
                step(dve.scalar_tensor_tensor(out=CW[:, tiles(g), 1], in0=PK[:, 1, :], scalar=0.5, in1=WZ[:, :],
                                              op0=ALU.mult, op1=ALU.mult))

            def table(ph):
                n = TG * GROUPS + 1
                step(dve.tensor_tensor(CNT[:, :], BT[:, 0, :], REG0, ALU.subtract))
                cmp = CMP[:, :].rearrange("p (e k) -> p e k", k=n)
                step(dve.tensor_tensor(cmp, CNT[:, :].unsqueeze(2).broadcast_to([P, E, n]),
                                       KTH.rearrange("p (e k) -> p e k", k=n), ALU.is_gt))
                step(dve.tensor_reduce(NT[:, :], cmp, AX_X, ALU.add))
                tri = CMP[:, 0:E * E].rearrange("p (e f) -> p e f", f=E)
                step(dve.tensor_tensor(tri, NT[:, :].unsqueeze(1).broadcast_to([P, E, E]),
                                       TRI.rearrange("p (e f) -> p e f", f=E), ALU.mult))
                step(dve.tensor_reduce(END[:, :], tri, AX_X, ALU.add))
                slt = SLT[:, :].rearrange("p (s e) -> p s e", e=E)
                step(dve.tensor_tensor(slt, SIOTA.rearrange("p (s e) -> p s e", e=E),
                                       END[:, :].unsqueeze(1).broadcast_to([P, SLOTS, E]), ALU.is_ge))
                step(dve.tensor_reduce(EID[:, :], slt, AX_X, ALU.add))
                step(dve.tensor_tensor(slt, slt, NT[:, :].unsqueeze(1).broadcast_to([P, SLOTS, E]), ALU.mult))
                step(dve.tensor_reduce(ST0[:, :], slt, AX_X, ALU.add))
                step(dve.tensor_tensor(ST0[:, :], SROW, ST0[:, :], ALU.subtract))
                step(dve.tensor_scalar(ST0[:, :], ST0[:, :], float(P), None, ALU.mult))
                step(dve.scalar_tensor_tensor(out=ST0[:, :], in0=EID[:, :], scalar=float(REGION), in1=ST0[:, :],
                                              op0=ALU.mult, op1=ALU.add))
                step(dve.tensor_copy(ROWI[:, :], ST0[:, :]))
                step(dve.tensor_scalar(EID[:, :], EID[:, :], float(E - 1), float(EW), ALU.min, ALU.mult))
                step(dve.tensor_copy(WOFI[:, :], EID[:, :]))
                dve.tensor_copy(TAILI[:, :], BT[:, 0, :]).then_inc(table_ready, 1)
                dve.wait_ge(table_ready, ph + 1)
                step(dve.tensor_copy(BT[:, 0, :], REG0))
                step(dve.tensor_tensor(END[:, :], END[:, :], NT[:, :], ALU.subtract))
                step(dve.scalar_tensor_tensor(out=END[:, :], in0=END[:, :], scalar=float(P), in1=REG0,
                                              op0=ALU.mult, op1=ALU.subtract))
                step(dve.tensor_tensor(OHD[:, :, :], OH[:, :, :, :].rearrange("p c t e -> p (c t) e"),
                                       END[:, :].unsqueeze(1).broadcast_to([P, TOPK * T, E]), ALU.mult))
                step(dve.tensor_reduce(YOFF[:, :], OHD[:, :, :], AX_X, ALU.add))
                step(dve.tensor_tensor(YOFF[:, :], YOFF[:, :], ROWF[:, :, :].rearrange("p c t -> p (c t)"), ALU.add))
                step(dve.tensor_copy(POSI[:, 0:T, :].rearrange("p t c -> p c t"),
                                     YOFF[:, :].rearrange("p (c t) -> p c t", c=TOPK)))
                dve.tensor_copy(POSI[:, T:T + TG, :], POSI[:, T - TG:T, :]).then_inc(posi_ready, 1)

            def ffn(ph):
                b = SLOTS * ph

                def gate(s, r):
                    dve.wait_ge(gelu_done, b + s + 1)
                    need(dve, at_done, b + s - 1)
                    dve.tensor_tensor(AV[r % 2][:, :], HPS[r % 2][:, HID:GW], GA[r % 2][:, :], ALU.mult)\
                        .then_inc(av_ready, 1)

                def result(s, r, i):
                    dve.wait_ge(y_done, b + s + 1)
                    if r % RING == 0:
                        need(dve, ys_out[r // RING], 16 * (i + SLOTS // XRING * ph))
                    dve.tensor_copy(YO[r // RING][:, r % RING, :], YPS[r % 2]).then_inc(yo_ready, 1)

                def ffn_step(s, r, i):
                    fixed = isinstance(s, int)
                    if not (fixed and s >= SLOTS):
                        gate(s, r)
                    if not (fixed and s < 2):
                        result(s - 2, (r - 2) % XRING, i if r >= 2 else i - 1)

                for s in range(XRING):
                    ffn_step(s, s, 0)
                with dve.Fori(1, SLOTS // XRING - 1) as i:
                    for r in range(XRING):
                        ffn_step(i * XRING + r, r, i)
                for s in range(SLOTS - XRING, SLOTS + 2):
                    ffn_step(s, s % XRING, s // XRING)

            def combine(g, k, used):
                dve.wait_ge(gathered, 16 * TG * TOPK * (k + 1))
                for c in range(TOPK):
                    for i in range(TG):
                        xt = X[:, g * TG + i, :]
                        last = c == TOPK - 1 and i == TG - 1
                        if i == 0 or last:
                            step.wait()
                        dve.scalar_tensor_tensor(out=xt, in0=YG[:, i, c, :], scalar=CW[:, g * TG + i, c:c + 1],
                                                 in1=xt, op0=ALU.mult, op1=ALU.add)\
                            .then_inc(yg_used if last else dve_step, 1)
                        step.n += not last
                dve.wait_ge(yg_used, used + 1)

            def mask_queries(g, j):
                k = g * UNITS + j
                if j % UNITS == 0:
                    dve.wait_ge(q_ready, g + 1)
                need(dve, s_done, k - 1)
                dve.tensor_tensor(QM[j % 2][:, :, :, :].rearrange("p a h q -> p (a h) q"),
                                  QT[:, g, j * W:(j + 1) * W].unsqueeze(1).broadcast_to([P, H, W]),
                                  HMASK.unsqueeze(2).broadcast_to([P, H, W]), ALU.mult).then_inc(qm_ready, 1)

            def attend(g, j):
                k = g * UNITS + j

                def of(lag):
                    return not isinstance(k, int) or 0 <= k - lag < GROUPS * UNITS

                if on(g + 1) and j == 5:
                    values(g + 1, 1)
                if of(4) and j % 2 == 1:
                    t = g * TG + (j - 5) // 2
                    dve.wait_ge(pj_done, t + 1)
                    dve.tensor_tensor(X[:, t, :], M0[:, 0:D], X[:, t, :], ALU.add).then_inc(res_done, 1)
                if of(0):
                    c = j % C
                    keys = slice(W if c == 0 else 0, 2 * W)
                    n = W if c == 0 else 2 * W
                    dve.wait_ge(s_done, k + 1)
                    step(dve.tensor_reduce(MX[j % 2][:, :], SPS[j % 2][:, :, keys], AX_X, ALU.max))
                    need(dve, t_done, k - C + 1)
                    dve.tensor_tensor(PR[c][:, :, keys], SPS[j % 2][:, :, keys],
                                      MX[j % 2][:, :].unsqueeze(2).broadcast_to([P, NP, n]), ALU.subtract)\
                        .then_inc(d_ready, 1)
                if on(g + 1) and j == 4:
                    values(g + 1, 0)
                if of(3):
                    dve.wait_ge(pv_done, k - 2)
                    o = M0[:, 0:NP * VW].rearrange("p (a v) -> p a v", v=VW)
                    step(dve.reciprocal(RD[:, :], o[:, :, 2 * DH]))
                    need(dve, ot_done, k - 3)
                    for h in range(2):
                        hp = slice(h * W, (h + 1) * W)
                        dve.tensor_tensor(OS[hp, h, :, :], o[hp, :, h * DH:(h + 1) * DH],
                                          RD[hp, :].unsqueeze(2).broadcast_to([W, NP, DH]), ALU.mult).then_inc(o_ready, 1)
                if on(g + 1) and j == 0:
                    combine(g + 1, g + 1, g + 1)
                if on(g - 1) and j == 3:
                    dve.wait_ge(res_done, g * TG)
                if of(-1):
                    mask_queries(g if j < UNITS - 1 else g + 1, (j + 1) % UNITS)
                if on(g + 1):
                    prep(g + 1, j)
                if on(g - 1):
                    kr = GROUPS + g - 1
                    if j == 3:
                        row_stats(g - 1, BST)
                        moments(RT, TG).then_inc(var_ready, 1)
                    if j == 4:
                        dve.wait_ge(rstd_ready, g + 1)
                        need(dve, scattered[0], 16 * 8 * (GROUPS // 2) + 16 * 8 * (g - 1))
                        for i in range(TG):
                            normalise(XN[0], (g - 1) * TG + i, i, RT, slice(i, i + 1)).then_inc(xn_ready, 1)
                    if j == 6:
                        dve.wait_ge(stok_ready, g + 1)
                        choose(kr, g - 1, RT["stok"][:, :])
                    if j == 7:
                        place(kr, g - 1, 0)

            def prep(g, j):
                if j == 0:
                    row_stats(g, BST)
                    moments(LN, TG).then_inc(lnvar_ready, 1)
                if j == 1:
                    dve.wait_ge(lnrstd_ready, g + 1)
                    need(dve, xat_done, g)
                    for i in range(TG):
                        if i == TG - 1:
                            step.wait()
                        ins = normalise(XA, g * TG + i, i, LN, slice(i, i + 1))
                        if i < TG - 1:
                            step.later(ins)
                    ins.then_inc(xa_ready, 1)
                    dve.wait_ge(xa_ready, g + 1)
                    step(dve.tensor_tensor(X[:, tiles(g), :], X[:, tiles(g), :],
                                           BO[:, :].unsqueeze(1).broadcast_to([P, TG, D]), ALU.add))
            def values(g, half):
                dve.wait_ge(v_done, g * 2 + half + 1)
                dve.tensor_tensor(V[:, bass.ds(g * UNITS + half * C, C), :, 0:2 * DH],
                                  M1.rearrange("p (w a v) -> p w a v", w=C, a=NP),
                                  BV[:, :].rearrange("p (a v) -> p a v", a=NP).unsqueeze(1)
                                  .broadcast_to([P, C, NP, 2 * DH]), ALU.add).then_inc(v_ready, 1)

            dve.wait_ge(w_loaded, 16 * WEIGHT_LOADS)
            step.later(dve.memset(XAT[:, :, 0:W], 0.0))
            step.later(dve.memset(KT[:, :, 0:W], 0.0))
            step.later(dve.memset(PR[0][:, :, 0:W], 0.0))
            step.later(dve.memset(OS[:, :, :, :], 0.0))
            step.later(dve.memset(V[:, :, :, 2 * DH:VW], 1.0))
            step(dve.tensor_copy(BT[:, 0, :], REG0))
            dve.tensor_scalar(RWS[:, :], RW[:, :], RS[:, :], float(D) ** -0.5, ALU.mult, ALU.mult).then_inc(consts_set, 1)
            for h in range(2):
                dve.wait_ge(x_loaded[h], 16)
                with dve.Fori(h * GROUPS // 2, (h + 1) * GROUPS // 2) as g:
                    step.enter(g, h * GROUPS // 2, TG)
                    row_stats(g, BST[:, tiles(g), :])
                    step.leave(GROUPS // 2)
            moments(ALL, T).then_inc(var_ready, 1)
            dve.wait_ge(rstd_ready, 1)

            for i in range(TG):
                normalise(XN[0], i, i, ALL, slice(i, i + 1)).then_inc(xn_ready, 1)
            dve.wait_ge(stok_ready, 1)

            def pair(i, last):
                for par in range(2):
                    k = i * 2 + par
                    if not (last and par == 1):
                        nx = 1 - par
                        need(dve, scattered[nx], (i + par) * (16 * TG * TOPK))
                        for t in range(TG):
                            normalise(XN[nx], (k + 1) * TG + t, t, ALL, bass.ds((k + 1) * TG + t, 1)).then_inc(xn_ready, 1)
                    choose(k, k, ALL["stok"][:, tiles(k)])
                    place(k, k, par)

            pair(0, False)
            with dve.Fori(1, GROUPS // 2 - 1) as i:
                step.enter(i, 1, 2 * STEPS_ROUTE)
                pair(i, False)
                step.leave(GROUPS // 2 - 2)
            pair(GROUPS // 2 - 1, True)
            table(0)
            ffn(0)
            combine(0, 0, 0)
            prep(0, 0)
            prep(0, 1)
            values(0, 0)
            values(0, 1)
            mask_queries(0, 0)
            for j in range(UNITS):
                attend(0, j)
            with dve.Fori(1, GROUPS - 1) as g:
                step.enter(g, 1, STEPS_GROUP)
                for j in range(UNITS):
                    attend(g, j)
                step.leave(GROUPS - 2)
            for g in range(GROUPS - 1, GROUPS + 1):
                for j in range(UNITS):
                    attend(g, j)
            table(1)
            ffn(1)
            with dve.Fori(0, GROUPS) as g:
                step.enter(g, 0, TOPK * TG - 1)
                combine(g, g + GROUPS + 1, g + GROUPS)
                step.leave(GROUPS)


STEPS_ROUTE = 27
STEPS_GROUP = 74


def kernel(L0_attn_x, L0_attn_Wq, L0_attn_bq, L0_attn_Wk, L0_attn_bk, L0_attn_Wv, L0_attn_bv, L0_attn_Wo,
           L0_attn_bo, L0_ffn_router_scale, L0_ffn_router_w, L0_ffn_gating_w, L0_ffn_linear_w,
           L0_ffn_per_expert_scale):
    import numpy as np
    import concourse.bacc as bacc
    from concourse.bass_utils import run_bass_kernel_spmd

    def rows(v):
        return np.ascontiguousarray(np.broadcast_to(np.asarray(v)[None, :], (P, len(v))))

    pair_order = np.arange(D).reshape(2, NP, DH).transpose(1, 0, 2).reshape(-1)
    gates = np.asarray(L0_ffn_gating_w).transpose(3, 0, 1, 2).reshape(P, E, GW)
    linear = np.asarray(L0_ffn_linear_w).reshape(E, 2, P, D).transpose(2, 0, 1, 3).reshape(P, E, 2 * D)
    part, n_k = np.arange(P), TG * GROUPS + 1
    head_mask = np.zeros((P, NP, 2))
    for c in range(P):
        head_mask[c, (c // DH) % NP, c // (NP * DH)] = 1
    consts = np.concatenate([
        np.eye(P), part[:, None] < part[None, :], np.ones((P, P)), head_mask.reshape(P, H),
        np.tile(E - np.arange(E), (P, 1)), np.tile(np.arange(E) * REGION, (P, 1)),
        np.tile(np.arange(n_k) * P, (P, E)), np.tile(np.repeat(np.arange(SLOTS), E), (P, 1)),
        np.tile((np.arange(E)[None, :] <= np.arange(E)[:, None]).reshape(-1), (P, 1)),
        np.tile(np.arange(SLOTS), (P, 1))], axis=1).astype(np.float32)
    arrays = dict(
        x=np.asarray(L0_attn_x).reshape(NSEQ * L, D),
        wq=np.asarray(L0_attn_Wq).T, bq=np.asarray(L0_attn_bq).reshape(P, 1),
        wk=np.asarray(L0_attn_Wk).T, bk=np.asarray(L0_attn_bk).reshape(P, 1),
        wv=np.asarray(L0_attn_Wv)[pair_order].T, bv=rows(np.asarray(L0_attn_bv)[pair_order]),
        wo=np.asarray(L0_attn_Wo).T, bo=rows(L0_attn_bo),
        rscale=np.asarray(L0_ffn_router_scale).reshape(P, 1), rw=np.asarray(L0_ffn_router_w),
        experts=np.concatenate([gates, linear], axis=2).reshape(P, E * EW),
        pes=rows(L0_ffn_per_expert_scale), consts=consts)
    arrays = {n: np.ascontiguousarray(a) for n, a in arrays.items()}
    nc = bacc.Bacc("TRN2", target_bir_lowering=False, num_devices=1)
    aps = {n: nc.dram_tensor(n, a.shape, F32, kind="ExternalInput").ap() for n, a in arrays.items()}
    out = nc.dram_tensor("out", (NSEQ * L, D), F32, kind="ExternalOutput").ap()
    macaron(nc, out=out, **aps)
    r = run_bass_kernel_spmd(nc, [arrays], core_ids=[0])
    return np.asarray(r.results[0]["out"]).reshape(NSEQ, L, D)
```

```python
from contextlib import ExitStack

import concourse.bass as bass
from concourse import mybir

F32 = mybir.dt.float32
I32 = mybir.dt.int32
U32 = mybir.dt.uint32
ALU = mybir.AluOpType
ACT = mybir.ActivationFunctionType
AX_X = mybir.AxisListType.X

P = 128
NSEQ, L, D = 16, 256, 128
T = NSEQ * L // P
TG = 4
GROUPS = T // TG
H, DH, W = 16, 8, 64
NP = H // 2
C = L // W
UNITS = TG * P // W
SLOT = 32
PAIRS, SIDES = P // SLOT, NP * SLOT // P
BIASED = 4
HALF = P // 2
HP = NP // 2
PADL = W + L
E, HID, TOPK = 8, 256, 2
GW = 2 * HID
EW = GW + 2 * D
REGION = NSEQ * L + P
SLOTS = 72
SPARE = SLOTS - NSEQ * L * TOPK // P + 1
ROWS = E * REGION + SPARE * P
FILLERS = E + SPARE
PARTS = 4
RING = 4
XRING = 2 * RING
CLAMPED = "computed on chip from counts that add up to the tokens, and clamped"
SCALE = float(DH) ** -0.5
LN_EPS, RMS_EPS = 1e-5, 1e-6


def need(eng, sem, value):
    if not (isinstance(value, int) and value <= 0):
        eng.wait_ge(sem, value)


class Steps:

    def __init__(self, eng, sem):
        self.eng, self.sem, self.base, self.n = eng, sem, 0, 0

    def __call__(self, ins):
        self.n += 1
        ins.then_inc(self.sem, 1)
        self.eng.wait_ge(self.sem, self.base + self.n)

    def later(self, ins):
        self.n += 1
        ins.then_inc(self.sem, 1)

    def wait(self):
        self.eng.wait_ge(self.sem, self.base + self.n)

    def enter(self, index, first, per):
        self.outside = self.base + self.n
        self.base, self.n, self.per = self.outside + (index - first) * per, 0, per

    def leave(self, times):
        assert self.n == self.per, f"steps in the body: {self.n}, not {self.per}"
        self.base, self.n = self.outside + times * self.per, 0


def macaron(nc, x, wq, bq, wk, bk, wv, bv, wo, bo, rscale, rw, experts, pes, consts, out):
    xs = nc.dram_tensor("xs_rows", [ROWS, D + 1], F32, kind="Internal").ap()
    ys = nc.dram_tensor("ys_rows", [TOPK * NSEQ * L + FILLERS * P, D], F32, kind="Internal").ap()
    x_tiles = x.rearrange("(t p) d -> p t d", p=P)
    out_tiles = out.rearrange("(t p) d -> p t d", p=P)
    ys_tiles = ys[0:TOPK * NSEQ * L, :].rearrange("(c t p) d -> p c t d", c=TOPK, p=P)

    with ExitStack() as ctx:
        def sb(name, shape, dt=F32):
            return ctx.enter_context(nc.sbuf_tensor(name, shape, dt))

        def sem(name):
            return ctx.enter_context(nc.semaphore(name))

        X = sb("X", [P, T, D])
        EXP = sb("EXP", [P, E * EW])
        WQ, WK, WV, WO = [sb(name, [P, D]) for name in ("WQ", "WK", "WV", "WO")]
        BQ, BK = sb("BQ", [P, 1]), sb("BK", [P, 1])
        BQS = sb("BQS", [P, 1])
        BV, BO = sb("BV", [P, D]), sb("BO", [P, D])
        RS, RW, RWS = sb("RS", [P, 1]), sb("RW", [P, E]), sb("RWS", [P, E])
        PES = sb("PES", [P, E])
        CN = sb("CN", [P, consts.shape[1]])
        o = 0
        parts = []
        for n in (P, P, P, NP, E, E, E * (TG * GROUPS + 1), SLOTS * E, E * E, SLOTS, T, FILLERS):
            parts.append(CN[:, o:o + n])
            o += n
        IDN, BEFORE, ONES, QMASK, IOTA, REG0, KTH, SIOTA, TRI, SROW, TOKEN, FROW = parts
        Q = sb("Q", [P, 2, C, HP, 2, W])
        K = sb("K", [P, 2, PADL])
        QS = sb("QS", [P, L])
        V = sb("V", [P, 2 * C, NP, SLOT])
        CW = sb("CW", [P, T, TOPK])
        NHALF, REPS, EULER = sb("NHALF", [P, T]), sb("REPS", [P, T]), sb("EULER", [P, T])
        FILL = sb("FILL", [P, FILLERS, D + 1])
        ALL, LN, RT = [{m: sb(f"{m}_{which}", [P, n]) for m in ("mean", "var", "vareps", "rstd", "msq", "stok")}
                       for which, n in (("all", T), ("ln", TG), ("rt", TG))]
        BST = sb("BST", [P, T // PARTS, 6])
        MSUM, MDIF, M2S = [sb(name, [P, T // PARTS]) for name in ("MSUM", "MDIF", "M2S")]
        XN = sb("XN", [P, TOPK, GROUPS, TG, D + 1])
        XNT = sb("XNT", [P, TG * P])
        LGS, TOP = sb("LGS", [P, TG, E]), sb("TOP", [P, TG, E])
        TIX, IXF = sb("TIX", [P, TG, E], U32), sb("IXF", [P, TOPK, TG])
        OH = sb("OH", [P, TOPK, T, E])
        IND = sb("IND", [P, TG, E])
        DL, EX, WZ = sb("DL", [P, T]), sb("EX", [P, T]), sb("WZ", [P, T])
        OHP, PK = sb("OHP", [P, TOPK, TG, E]), sb("PK", [P, TOPK * T])
        BT = sb("BT", [P, TG + 1, E])
        PX = sb("PX", [P, 2 * TG, E])
        POSM = sb("POSM", [P, TG, E])
        OHD = sb("OHD", [P, TOPK * T, E])
        ROWF = sb("ROWF", [P, TOPK, TG])
        IDX = sb("IDX", [P, GROUPS, TOPK, TG], U32)
        YG = [sb(f"YG{i}", [P, TOPK, TG, D]) for i in range(2)]
        CNT, NT, END = sb("CNT", [P, E]), sb("NT", [P, E]), sb("END", [P, E])
        CMP = sb("CMP", [P, E * (TG * GROUPS + 1)])
        SLT = sb("SLT", [P, SLOTS * E])
        EID, ST0 = sb("EID", [P, SLOTS]), sb("ST0", [P, SLOTS])
        ROWI, WOFI, TAILI = sb("ROWI", [P, SLOTS], I32), sb("WOFI", [P, SLOTS], I32), sb("TAILI", [P, E], I32)
        XS = sb("XS", [P, XRING, D + 1])
        XST = [sb(f"XST{i}", [P, P]) for i in range(2)]
        GA = [sb(f"GA{i}", [P, HID]) for i in range(2)]
        AV = [sb(f"AV{i}", [P, HID]) for i in range(2)]
        AVT = [sb(f"AVT{i}", [P, HID]) for i in range(2)]
        YO = sb("YO", [P, XRING, D])
        XA = sb("XA", [P, TG, D])
        XAT = sb("XAT", [P, 2, PADL])
        MX = [sb(f"MX{i}", [P, NP]) for i in range(2)]
        PR = [sb(f"PR{i}", [P, NP, 2 * W]) for i in range(C)]
        PT = [sb(f"PT{i}", [P, NP, P]) for i in range(2)]
        PVS = sb("PVS", [P, SIDES, P])
        RD = sb("RD", [P, NP])
        OS = sb("OS", [P, 2, 2, NP, DH])
        OT = sb("OT", [P, 2, W])

        PS = ctx.enter_context(nc.psum_tensor("PS", [P, 8, 512], F32))
        HPS = [PS[:, i, :] for i in range(2)]
        XTP = [PS[:, 2 + i, 0:P] for i in range(2)]
        ATP = [PS[:, 4 + i, 0:HID] for i in range(2)]
        YPS = [PS[:, 6 + i, 0:D] for i in range(2)]
        SPS = [PS[:, 2 * i:2 * i + 2, :].rearrange("p a (b k) -> p (a b) k", k=P) for i in range(2)]
        TPS = PS[:, 4, :].rearrange("p (b k) -> p b k", k=P)
        OPS, PVP, M1 = PS[:, 5, :], PS[:, 6, :], PS[:, 7, :]
        ROUTER = [[PS[:, 4, :], PS[:, 5, :], PS[:, 6, :]], [M1] * 3]

        x_loaded = [sem(f"x_loaded{h}") for h in range(PARTS)]
        w_loaded, e_loaded, xs_zeroed = sem("w_loaded"), sem("e_loaded"), sem("xs_zeroed")
        consts_set = sem("consts_set")
        pool_consts = sem("pool_consts")
        dve_step, act_step, pool_step = sem("dve_step"), sem("act_step"), sem("pool_step")
        var_ready, rstd_ready, stok_ready = sem("var_ready"), sem("rstd_ready"), sem("stok_ready")
        diff_ready, exp_ready = sem("diff_ready"), sem("exp_ready")
        xn_ready, rt_done, xnt_ready = sem("xn_ready"), sem("rt_done"), sem("xnt_ready")
        lg_done, ind_ready, px_done = sem("lg_done"), sem("ind_ready"), sem("px_done")
        lg_used, px_used = sem("lg_used"), sem("px_used")
        idx_ready = sem("idx_ready")
        scattered = sem("scattered")
        tails_ready = sem("tails_ready")
        table_ready, tails_zeroed = sem("table_ready"), sem("tails_zeroed")
        xs_in = [sem(f"xs_in{i}") for i in range(XRING)]
        ys_out = [sem(f"ys_out{i}") for i in range(XRING)]
        xt_done, xst_ready, h_done = sem("xt_done"), sem("xst_ready"), sem("h_done")
        gelu_done, av_ready, at_done = sem("gelu_done"), sem("av_ready"), sem("at_done")
        avt_ready, y_done, yo_ready = sem("avt_ready"), sem("y_done"), sem("yo_ready")
        yg_in, yg_used = [sem(f"yg_in{i}") for i in range(2)], sem("yg_used")
        fill_ready, xn2_ready = sem("fill_ready"), sem("xn2_ready")
        lnvar_ready, lnrstd_ready = sem("lnvar_ready"), sem("lnrstd_ready")
        xa_ready, xat_done, xat_ready = sem("xa_ready"), sem("xat_done"), sem("xat_ready")
        q_done, q_ready, k_done, k_ready = sem("q_done"), sem("q_ready"), sem("k_done"), sem("k_ready")
        v_done, v_ready = sem("v_done"), sem("v_ready")
        qm_ready, s_done, d_ready, p_ready = sem("qm_ready"), sem("s_done"), sem("d_ready"), sem("p_ready")
        b_ready = sem("b_ready")
        pvs_ready, r_done = sem("pvs_ready"), sem("r_done")
        t_done, pt_ready, pv_done, o_ready = sem("t_done"), sem("pt_ready"), sem("pv_done"), sem("o_ready")
        ot_done, ot_ready, pj_done, res_done = sem("ot_done"), sem("ot_ready"), sem("pj_done"), sem("res_done")
        stored, groups_sent, tiles_sent = sem("stored"), sem("groups_sent"), sem("tiles_sent")

        WEIGHT_LOADS = 12

        def tiles(g, n=TG):
            return bass.ds(g * TG, n)

        def on(g):
            return not isinstance(g, int) or 0 <= g < GROUPS

        def part_tiles(h):
            return slice(h * T // PARTS, (h + 1) * T // PARTS)

        def unit_on(k):
            return not isinstance(k, int) or 0 <= k < GROUPS * UNITS

        def seq_on(s):
            return not isinstance(s, int) or 0 <= s < NSEQ

        def stage_sequence(g, j):
            ahead = {0: 1, 1: 0, 2: 2, 3: 2}[j % C]
            s = 2 * g + j // C + ahead
            return s, (j // C + ahead) % 2

        block = ctx.enter_context(nc.Block())

        @block.sync
        def _(sp):
            for h in range(PARTS):
                sp.dma_start(X[:, part_tiles(h), :], x_tiles[:, part_tiles(h), :]).then_inc(x_loaded[h], 16)
            for dst, src in ((CN, consts), (RS, rscale), (RW, rw), (PES, pes), (WQ, wq), (WK, wk), (WV, wv),
                             (BQ, bq), (BK, bk), (BV, bv), (BO, bo)):
                sp.dma_start(dst[:, :], src).then_inc(w_loaded, 16)
            sp.dma_start(WO[:, :], wo).then_inc(w_loaded, 16)
            sp.dma_start(EXP[:, :], experts).then_inc(e_loaded, 16)
            sp.wait_ge(fill_ready, 1)
            sp.dma_start(xs[E * REGION:ROWS, :].rearrange("(n p) d -> p n d", p=P), FILL[:, E:, :]).then_inc(xs_zeroed, 16)

            def row_at(reg, entry, high):
                sp.load(reg, entry)
                return nc.s_assert_within(sp.snap(reg), min_val=0, max_val=high, skip_runtime_bounds_check_because=CLAMPED)

            row_regs = [sp.alloc_register(f"row{r}") for r in range(XRING)]

            def ffn(ph):
                sp.wait_ge(tails_ready, ph + 1)
                for e in range(E):
                    r = row_at(row_regs[e], TAILI[0:1, e:e + 1], ROWS - P)
                    sp.dma_start(xs[bass.ds(r, P), :], FILL[:, e, :]).then_inc(tails_zeroed, 16)
                sp.wait_ge(table_ready, ph + 1)
                sp.wait_ge(tails_zeroed, 16 * E * (ph + 1))
                sp.wait_ge(xs_zeroed, 16)
                sp.wait_ge(scattered, 16 * TG * TOPK * GROUPS * (ph + 1))

                def load(i, r):
                    need(sp, ys_out[r], 16 * (i + SLOTS // XRING * ph))
                    row = row_at(row_regs[r], ROWI[0:1, bass.ds(i * XRING + r, 1)], ROWS - P)
                    sp.dma_start(XS[:, r, :], xs[bass.ds(row, P), :]).then_inc(xs_in[r], 16)

                for r in range(XRING):
                    load(0, r)
                with sp.Fori(1, SLOTS // XRING) as i:
                    for r in range(XRING):
                        load(i, r)
                for r in range(XRING):
                    sp.wait_ge(ys_out[r], 16 * (SLOTS // XRING) * (ph + 1))

            def load_results(g, place):
                for c in range(TOPK):
                    sp.dma_start(YG[place][:, c, :, :], ys_tiles[:, c, tiles(g), :]).then_inc(yg_in[place], 16)

            def store_group(g):
                sp.wait_ge(yg_used, GROUPS + g + 1)
                sp.dma_start(out_tiles[:, tiles(g), :], X[:, tiles(g), :]).then_inc(stored, 16)

            ffn(0)
            load_results(0, 0)
            with sp.Fori(1, GROUPS) as g:
                sp.wait_ge(yg_used, g)
                load_results(g, 0)
            ffn(1)
            for par in range(2):
                load_results(par, par)
            with sp.Fori(0, GROUPS // 2 - 1) as i:
                for par in range(2):
                    store_group(i * 2 + par)
                    load_results(i * 2 + par + 2, par)
            for par in range(2):
                store_group(GROUPS - 2 + par)
            sp.wait_ge(stored, 16 * GROUPS)

        @block.gpsimd
        def _(pool):
            pool.memset(FILL[:, :, :], 0.0).then_inc(pool_consts, 1)
            step = Steps(pool, pool_step)
            step.later(pool.memset(NHALF[:, :], -0.5))
            step.later(pool.memset(REPS[:, :], RMS_EPS))
            step(pool.memset(EULER[:, :], 2.718281828459045))

            def router_scales(st, at, done):
                rstd, msq, stok, n = st["rstd"][:, at], st["msq"][:, at], st["stok"][:, at], at.stop - at.start
                pool.tensor_tensor(rstd, st["vareps"][:, at], NHALF[:, 0:n], ALU.pow).then_inc(rstd_ready, 1)
                pool.wait_ge(rstd_ready, done + 1)
                step(pool.tensor_tensor(msq, rstd, rstd, ALU.mult))
                step(pool.tensor_tensor(msq, msq, st["var"][:, at], ALU.mult))
                step(pool.tensor_tensor(msq, msq, REPS[:, 0:n], ALU.add))
                pool.tensor_tensor(stok, msq, NHALF[:, 0:n], ALU.pow).then_inc(stok_ready, 1)

            def exponentials(ph):
                pool.wait_ge(diff_ready, GROUPS * (ph + 1))
                pool.tensor_tensor(EX[:, :], EULER[:, :], DL[:, :], ALU.pow).then_inc(exp_ready, 1)

            def route(k, place):
                pool.wait_ge(idx_ready, k + 1)
                pool.wait_ge(xn2_ready, k + 1)
                pool.sem_inc(groups_sent, 1)
                for i in range(TG):
                    for c in range(TOPK):
                        pool.indirect_dma_start(xs, bass.IndirectOffsetOnAxis(ap=IDX[:, place, c, i:i + 1], axis=0),
                                                XN[:, c, place, i, :], None).then_inc(scattered, 16)

            def results(ph):
                with pool.Fori(0, SLOTS // XRING) as i:
                    for r in range(XRING):
                        pool.wait_ge(yo_ready, SLOTS * ph + i * XRING + r + 1)
                        pool.sem_inc(tiles_sent, 1)
                        pool.indirect_dma_start(ys, bass.IndirectOffsetOnAxis(ap=XS[:, r, D:D + 1].bitcast(U32), axis=0),
                                                YO[:, r, :], None).then_inc(ys_out[r], 16)

            def part_scales(h):
                pool.wait_ge(var_ready, h + 1)
                router_scales(ALL, part_tiles(h), h)

            part_scales(0)
            part_scales(1)
            for k in range(GROUPS):
                route(k, k)
                if k % 2 == 0 and k // 2 + 2 < PARTS:
                    part_scales(k // 2 + 2)
            exponentials(0)

            def mask_queries(s, par):
                if seq_on(s):
                    pool.wait_ge(q_ready, s + 1)
                    need(pool, s_done, (s - 1) * C)
                    for c in range(C):
                        pool.tensor_tensor(Q[:, par, c, :, :, :].rearrange("p a h q -> p (a h) q"),
                                           QS[:, c * W:(c + 1) * W].unsqueeze(1).broadcast_to([P, NP, W]),
                                           QMASK.unsqueeze(2).broadcast_to([P, NP, W]), ALU.mult).then_inc(qm_ready, 1)

            def scales_of(g):
                pool.wait_ge(var_ready, PARTS + g)
                router_scales(RT, slice(0, TG), PARTS + g - 1)

            def body(g):
                mask_queries(2 * g + 1, 1)
                if on(g + 1):
                    pool.wait_ge(lnvar_ready, g + 2)
                    pool.tensor_tensor(LN["rstd"][:, :], LN["vareps"][:, :], NHALF[:, 0:TG], ALU.pow)\
                        .then_inc(lnrstd_ready, 1)
                mask_queries(2 * g + 2, 0)
                last_scales_first = isinstance(g, int) and g == GROUPS
                if last_scales_first:
                    scales_of(g)
                if on(g - 2):
                    route(GROUPS + g - 2, 1 if isinstance(g, int) and g == GROUPS + 1 else 0)
                if on(g - 1) and not last_scales_first:
                    scales_of(g)

            results(0)
            for g in range(-1, 2):
                body(g)
            with pool.Fori(2, GROUPS - 1) as g:
                step.enter(g, 2, 3)
                body(g)
                step.leave(GROUPS - 3)
            for g in range(GROUPS - 1, GROUPS + 2):
                body(g)
            exponentials(1)
            results(1)

        @block.tensor
        def _(pe):
            offsets = [pe.alloc_register(f"weight_offset{r}") for r in range(RING)]

            def transposes_of_router(k, place, bank):
                pe.wait_ge(xn_ready, TG * (k + 1))
                need(pe, xnt_ready, k)
                for i in range(TG):
                    ins = pe.transpose(bank[:, i * P:(i + 1) * P], XN[:, 0, place, i, 0:D], IDN)
                ins.then_inc(rt_done, 1)

            def logits(k, bank):
                need(pe, lg_used, k)
                pe.wait_ge(xnt_ready, k + 1)
                for i in range(TG):
                    ins = pe.matmul(bank[:, i * E:(i + 1) * E], XNT[:, i * P:(i + 1) * P], RWS[:, :],
                                    start=True, stop=True)
                ins.then_inc(lg_done, 1)

            def prefixes(k, bank):
                need(pe, px_used, k)
                pe.wait_ge(ind_ready, k + 1)
                ind = IND[:, :, :].rearrange("p t e -> p (t e)")
                pe.matmul(bank[:, 0:TG * E], BEFORE, ind, start=True, stop=True)
                pe.matmul(bank[:, TG * E:2 * TG * E], ONES, ind, start=True, stop=True).then_inc(px_done, 1)

            def ffn(ph):
                b = SLOTS * ph
                pe.wait_ge(table_ready, ph + 1)

                def transpose_in(s, r, rounds):
                    pe.wait_ge(xs_in[r], 16 * (rounds + 1 + SLOTS // XRING * ph))
                    need(pe, xst_ready, b + s - 1)
                    pe.transpose(XTP[r % 2], XS[:, r, 0:D], IDN).then_inc(xt_done, 1)

                def load_offset(s, r):
                    pe.load(offsets[r % RING], WOFI[0:1, bass.ds(s, 1)])

                def offset(r):
                    return nc.s_assert_within(pe.snap(offsets[r % RING]), min_val=0, max_val=(E - 1) * EW,
                                              skip_runtime_bounds_check_because=CLAMPED)

                def gates(s, r):
                    pe.wait_ge(xst_ready, b + s + 1)
                    need(pe, av_ready, b + s - 1)
                    pe.matmul(HPS[r % 2], XST[r % 2][:, :], EXP[:, bass.ds(offset(r), GW)], start=True, stop=True)\
                        .then_inc(h_done, 1)

                def down(s, r):
                    pe.wait_ge(avt_ready, b + s + 1)
                    need(pe, yo_ready, b + s - 1)
                    o = offset(r)
                    for c in range(2):
                        ins = pe.matmul(YPS[r % 2], AVT[r % 2][:, c * P:(c + 1) * P],
                                        EXP[:, bass.ds(o + (GW + c * D), D)], start=(c == 0), stop=(c == 1))
                    ins.then_inc(y_done, 1)

                def transpose_hidden(s, r):
                    pe.wait_ge(av_ready, b + s + 1)
                    need(pe, avt_ready, b + s - 1)
                    for c in range(2):
                        ins = pe.transpose(ATP[r % 2][:, c * P:(c + 1) * P], AV[r % 2][:, c * P:(c + 1) * P], IDN)
                    ins.then_inc(at_done, 1)

                def step(s, r, i):
                    fixed = isinstance(s, int)
                    if not (fixed and s >= SLOTS - 1):
                        transpose_in(s + 1, (r + 1) % XRING, i + (r + 1) // XRING)
                    if not (fixed and s >= SLOTS):
                        gates(s, r)
                    if not (fixed and s >= SLOTS - 1):
                        load_offset(s + 1, r + 1)
                    if not (fixed and s < 2):
                        down(s - 2, (r - 2) % XRING)
                    if not (fixed and (s < 1 or s > SLOTS)):
                        transpose_hidden(s - 1, (r - 1) % XRING)

                load_offset(0, 0)
                transpose_in(0, 0, 0)
                for s in range(XRING):
                    step(s, s, 0)
                with pe.Fori(1, SLOTS // XRING - 1) as i:
                    for r in range(XRING):
                        step(i * XRING + r, r, i)
                for s in range(SLOTS - XRING, SLOTS + 2):
                    step(s, s % XRING, s // XRING)

            def slot_a(g, j):
                s, par = stage_sequence(g, j)
                if not seq_on(s):
                    return
                if j % C == 2:
                    pe.wait_ge(xa_ready, g + 2)
                    need(pe, v_ready, s - 1)
                    if not seq_on(s - 2):
                        need(pe, k_ready, s)
                    if on(g - 2) and j == 2:
                        pe.wait_ge(lg_used, GROUPS + g - 1)
                    for i in range(L // P):
                        ins = pe.transpose(M1[:, i * P:(i + 1) * P], XA[:, par * 2 + i, :], IDN)
                    ins.then_inc(xat_done, 1)
                elif j % C == 1:
                    if seq_on(s + 1):
                        pe.wait_ge(k_ready, s + 2)
                    elif on(g - 2):
                        pe.wait_ge(px_used, GROUPS + g - 1)
                    if j == 1 and on(g - 2):
                        pe.wait_ge(xnt_ready, GROUPS + g - 1)
                    for c in range(C):
                        ins = pe.matmul(M1[:, c * P:(c + 1) * P], XAT[:, par, c * W:c * W + 2 * W], WV[:, :],
                                        start=True, stop=True)
                    ins.then_inc(v_done, 1)
                else:
                    if j % C == 3:
                        w, done = WQ, q_done
                        pe.wait_ge(xat_ready, s + 1)
                    else:
                        w, done = WK, k_done
                        pe.wait_ge(q_ready, s + 1)
                        if j == 4 and on(g - 2):
                            pe.wait_ge(px_used, GROUPS + g - 1)
                    pe.matmul(M1[:, 0:L], w[:, :], XAT[:, par, W:PADL], start=True, stop=True).then_inc(done, 1)

            def slot_b(g, j):
                k = GROUPS + g - 2
                if on(g - 2):
                    if j == 1:
                        if seq_on(2 * g + 1):
                            pe.wait_ge(k_ready, 2 * g + 2)
                        transposes_of_router(k, 1 if isinstance(g, int) and g == GROUPS + 1 else 0, M1)
                    if j == 2:
                        if seq_on(2 * g):
                            pe.wait_ge(v_ready, 2 * g + 1)
                        logits(k, M1)
                    if j == 4:
                        if seq_on(2 * g + 2):
                            pe.wait_ge(q_ready, 2 * g + 3)
                        prefixes(k, M1)

            def scores(g, j, half):
                c, par = j % C, j // C % 2
                first = 1 if c == 0 else 0
                rows = slice(half * HALF, (half + 1) * HALF)
                for p in range(HP):
                    ins = pe.matmul(SPS[j % 2][:, half * HP + p, first * W:2 * W], Q[rows, par, c, p, :, :],
                                    K[rows, par, (c + first) * W:(c + 2) * W], start=True, stop=True)
                return ins

            def attend(g, j):
                k = g * UNITS + j

                def of(lag):
                    return unit_on(k - lag)

                def transpose_probabilities(half):
                    for p in range(HP):
                        ins = pe.transpose(TPS[:, p, :], PR[(j - 2) % C][:, half * HP + p, :], IDN)
                    ins.then_inc(t_done, 1)

                def last_output_read():
                    if of(6):
                        pe.wait_ge(ot_ready, k - 5)
                    else:
                        need(pe, o_ready, 2 * (k - 4))

                if of(4):
                    pe.wait_ge(pvs_ready, k - 3)
                    last_output_read()
                    for i in range(SIDES):
                        ins = pe.transpose(OPS[:, i * P:(i + 1) * P], PVS[:, i, :], IDN)
                    ins.then_inc(r_done, 1)
                if of(-1):
                    if (j + 1) % C == 0:
                        pe.wait_ge(k_ready, 2 * g + (j + 1) // C + 1)
                    pe.wait_ge(qm_ready, k + 2)
                    need(pe, d_ready, k)
                    scores(g, j + 1, 0)
                if of(7) and j % 2 == 1:
                    pe.wait_ge(ot_ready, k - 5)
                    if not of(4):
                        pe.wait_ge(pvs_ready, GROUPS * UNITS)
                        pe.wait_ge(res_done, g * TG + (j - 7) // 2)
                    pe.matmul(PVP[:, 0:D], OT[:, :, :], WO[:, :], start=True, stop=True).then_inc(pj_done, 1)
                if of(2):
                    pe.wait_ge(p_ready, k - 1)
                    need(pe, pt_ready, 2 * (k - 2))
                    transpose_probabilities(0)
                if of(-1):
                    need(pe, b_ready, k)
                    scores(g, j + 1, 1).then_inc(s_done, 1)
                if of(5):
                    if of(4):
                        pe.wait_ge(o_ready, 2 * (k - 3))
                    else:
                        pe.wait_ge(o_ready, 2 * (k - 4))
                        last_output_read()
                    pe.transpose(OPS[:, 0:P], OS[:, (j - 1) % 2, :, :, :].rearrange("p h a d -> p (h a d)"), IDN)\
                        .then_inc(ot_done, 1)
                slot_b(g, j)
                if of(2):
                    pe.wait_ge(pt_ready, 2 * (k - 2) + 1)
                    transpose_probabilities(1)
                if of(3):
                    pe.wait_ge(pt_ready, 2 * (k - 2))
                    if (j - 3) % C == 0:
                        pe.wait_ge(v_ready, 2 * g + (j - 3) // C + 1)
                    need(pe, pvs_ready, k - 3)
                    if of(7) and j % 2 == 1:
                        pe.wait_ge(res_done, g * TG + (j - 7) // 2 + 1)
                    for p in range(NP):
                        i, rows = p // PAIRS, slice(p % PAIRS * SLOT, (p % PAIRS + 1) * SLOT)
                        ins = pe.matmul(PVP[rows, i * P:(i + 1) * P], V[:, (j - 3) % UNITS, p, :],
                                        PT[(j - 3) % 2][:, p, :], start=True, stop=True)
                    ins.then_inc(pv_done, 1)
                slot_a(g, j)

            pe.wait_ge(w_loaded, 16 * WEIGHT_LOADS)
            pe.wait_ge(consts_set, 1)
            rows_bank, logits_bank, prefixes_bank = ROUTER[0]
            for k in range(GROUPS + 1):
                if k < GROUPS:
                    transposes_of_router(k, k, rows_bank)
                    logits(k, logits_bank)
                if k > 0:
                    prefixes(k - 1, prefixes_bank)
            need(pe, px_used, GROUPS)
            pe.wait_ge(e_loaded, 16)
            ffn(0)
            pe.wait_ge(avt_ready, SLOTS)
            pe.wait_ge(yo_ready, SLOTS)
            for g in range(-1, 2):
                for j in range(UNITS):
                    attend(g, j)
            with pe.Fori(2, GROUPS - 1) as g:
                for j in range(UNITS):
                    attend(g, j)
            for g in range(GROUPS - 1, GROUPS + 2):
                for j in range(UNITS):
                    attend(g, j)
            pe.wait_ge(px_used, 2 * GROUPS)
            ffn(1)

        @block.scalar
        def _(act):
            def router_rows(k, place, bank):
                act.wait_ge(rt_done, k + 1)
                need(act, lg_done, k)
                act.copy(XNT[:, :], bank).then_inc(xnt_ready, 1)
                act.copy(XN[:, 1, place, :, 0:D], XN[:, 0, place, :, 0:D]).then_inc(xn2_ready, 1)

            def ffn(ph):
                b = SLOTS * ph

                def rows(s, r):
                    act.wait_ge(xt_done, b + s + 1)
                    need(act, h_done, b + s - 1)
                    act.copy(XST[r % 2][:, :], XTP[r % 2]).then_inc(xst_ready, 1)

                def gelu(s, r):
                    act.wait_ge(h_done, b + s + 1)
                    need(act, av_ready, b + s - 1)
                    act.activation(GA[r % 2][:, :], HPS[r % 2][:, 0:HID], ACT.Gelu_apprx_tanh).then_inc(gelu_done, 1)

                def acts(s, r):
                    act.wait_ge(at_done, b + s + 1)
                    need(act, y_done, b + s - 1)
                    act.copy(AVT[r % 2][:, :], ATP[r % 2]).then_inc(avt_ready, 1)

                def step(s, r):
                    fixed = isinstance(s, int)
                    if not (fixed and s > SLOTS - 2):
                        rows(s + 1, (r + 1) % RING)
                    if not (fixed and s >= SLOTS):
                        gelu(s, r)
                    if not (fixed and s < 1):
                        acts(s - 1, (r - 1) % RING)

                rows(0, 0)
                for s in range(RING):
                    step(s, s)
                with act.Fori(1, SLOTS // RING - 1) as i:
                    for r in range(RING):
                        step(i * RING + r, r)
                for s in range(SLOTS - RING, SLOTS + 1):
                    step(s, s % RING)

            def evict_a(g, j):
                s, par = stage_sequence(g, j)
                if not seq_on(s):
                    return
                if j % C == 2:
                    act.wait_ge(xat_done, s + 1)
                    need(act, v_done, s - 1)
                    act.copy(XAT[:, par, W:PADL], M1[:, 0:L]).then_inc(xat_ready, 1)
                if j % C == 3:
                    act.wait_ge(q_done, s + 1)
                    need(act, qm_ready, s * C)
                    act.activation(QS[:, :], M1[:, 0:L], ACT.Identity, bias=BQS[:, :], scale=SCALE).then_inc(q_ready, 1)
                if j % C == 0:
                    act.wait_ge(k_done, s + 1)
                    need(act, s_done, (s - 1) * C)
                    act.activation(K[:, par, W:PADL], M1[:, 0:L], ACT.Identity, bias=BK[:, :]).then_inc(k_ready, 1)

            def attend(g, j):
                k = g * UNITS + j

                def of(lag):
                    return unit_on(k - lag)

                if of(1):
                    c = (j - 1) % C
                    keys = slice(W if c == 0 else 0, 2 * W)
                    act.wait_ge(d_ready, k)
                    for p in range(NP - BIASED, NP):
                        ins = act.activation(PR[c][:, p, keys], SPS[(j - 1) % 2][:, p, keys], ACT.Exp,
                                             bias=MX[(j - 1) % 2][:, p:p + 1])
                    ins.then_inc(b_ready, 1)
                evict_a(g if j > 0 else g - 1, (j - 1) % UNITS)
                if of(1):
                    pr = PR[c][:, 0:NP - BIASED, keys]
                    act.activation(pr, pr, ACT.Exp).then_inc(p_ready, 1)
                def probabilities(half):
                    act.wait_ge(t_done, 2 * (k - 2) + half + 1)
                    need(act, pv_done, k - 3)
                    act.copy(PT[(j - 2) % 2][:, half * HP:(half + 1) * HP, :], TPS).then_inc(pt_ready, 1)

                if of(2):
                    probabilities(0)
                if of(5):
                    act.wait_ge(ot_done, k - 4)
                    if (j - 5) % 2 == 0:
                        need(act, pj_done, g * TG + (j - 5) // 2)
                    for h in range(2):
                        hp = slice(h * W, (h + 1) * W)
                        ins = act.copy(OT[hp, (j - 5) % 2, :], OPS[hp, h * W:(h + 1) * W])
                    ins.then_inc(ot_ready, 1)
                if on(g - 2) and j == 1:
                    router_rows(GROUPS + g - 2, 1 if isinstance(g, int) and g == GROUPS + 1 else 0, M1)
                if of(2):
                    probabilities(1)
                if of(3):
                    act.wait_ge(pv_done, k - 2)
                    need(act, r_done, k - 3)
                    act.copy(PVS[:, :, :], PVP[:, 0:SIDES * P].rearrange("p (i t) -> p i t", i=SIDES))\
                        .then_inc(pvs_ready, 1)

            act.wait_ge(w_loaded, 16 * WEIGHT_LOADS)
            act.mul(BQS[:, :], BQ[:, :], SCALE).then_inc(act_step, 1)
            act.wait_ge(act_step, 1)
            router_rows(0, 0, ROUTER[0][0])
            with act.Fori(1, GROUPS) as k:
                router_rows(k, k, ROUTER[0][0])
            ffn(0)
            for g in range(-1, 2):
                for j in range(UNITS):
                    attend(g, j)
            with act.Fori(2, GROUPS - 1) as g:
                for j in range(UNITS):
                    attend(g, j)
            for g in range(GROUPS - 1, GROUPS + 2):
                for j in range(UNITS):
                    attend(g, j)
            ffn(1)

        @block.vector
        def _(dve):
            step = Steps(dve, dve_step)

            def row_stats(g, bst):
                for i in range(TG):
                    step.later(dve.bn_stats(bst[:, i, :], X[:, g * TG + i, :]))

            def moments(st, at):
                n = at.stop - at.start
                m0, q0, m1, q1 = (BST[:, 0:n, i] for i in (1, 2, 4, 5))
                step.wait()
                step.later(dve.tensor_tensor(MSUM[:, 0:n], m0, m1, ALU.add))
                step.later(dve.tensor_tensor(MDIF[:, 0:n], m0, m1, ALU.subtract))
                step(dve.tensor_tensor(M2S[:, 0:n], q0, q1, ALU.add))
                step.later(dve.tensor_scalar(st["mean"][:, at], MSUM[:, 0:n], 0.5, None, ALU.mult))
                step(dve.scalar_tensor_tensor(out=MDIF[:, 0:n], in0=MDIF[:, 0:n], scalar=0.25, in1=MDIF[:, 0:n],
                                              op0=ALU.mult, op1=ALU.mult))
                step(dve.scalar_tensor_tensor(out=st["var"][:, at], in0=M2S[:, 0:n], scalar=1.0 / D, in1=MDIF[:, 0:n],
                                              op0=ALU.mult, op1=ALU.add))
                return dve.tensor_scalar(st["vareps"][:, at], st["var"][:, at], LN_EPS, None, ALU.add)

            def rows_of(k, g, place, st, column):
                for c in range(TOPK):
                    step.later(dve.tensor_scalar(XN[:, c, place, :, D].bitcast(U32), TOKEN[:, tiles(g)],
                                                 float(c * NSEQ * L), None, ALU.add))
                for i in range(TG):
                    normalise(XN[:, 0, place, i, 0:D], g * TG + i, st, column(i)).then_inc(xn_ready, 1)

            def normalise(dst, t, st, a):
                return dve.tensor_scalar(dst, X[:, t, :], st["mean"][:, a], st["rstd"][:, a],
                                         ALU.subtract, ALU.mult)

            def scale_logits(k, stok, bank):
                dve.wait_ge(lg_done, k + 1)
                dve.tensor_tensor(LGS[:, :, :], bank[:, 0:TG * E].rearrange("p (t e) -> p t e", e=E),
                                  stok.unsqueeze(2).broadcast_to([P, TG, E]), ALU.mult).then_inc(lg_used, 1)

            def choose(k, g):
                for i in range(TG):
                    step.later(dve.max(TOP[:, i, :], LGS[:, i, :]))
                step.wait()
                dve.tensor_tensor(DL[:, tiles(g)], TOP[:, :, 1], TOP[:, :, 0], ALU.subtract).then_inc(diff_ready, 1)
                for i in range(TG):
                    step.later(dve.max_index(TIX[:, i, :], TOP[:, i, :], LGS[:, i, :]))
                step.wait()
                step(dve.tensor_copy(IXF[:, :, :], TIX[:, :, 0:TOPK].rearrange("p t c -> p c t")))
                for c in range(TOPK):
                    step.later(dve.tensor_tensor(OH[:, c, tiles(g), :], IOTA.unsqueeze(1).broadcast_to([P, TG, E]),
                                                 IXF[:, c, :].unsqueeze(2).broadcast_to([P, TG, E]), ALU.is_equal))
                step.wait()
                dve.tensor_tensor(IND[:, :, :], OH[:, 0, tiles(g), :], OH[:, 1, tiles(g), :], ALU.add).then_inc(ind_ready, 1)

            def take_prefixes(k, bank):
                dve.wait_ge(px_done, k + 1)
                dve.tensor_copy(PX[:, :, :], bank[:, 0:2 * TG * E].rearrange("p (t e) -> p t e", e=E)).then_inc(px_used, 1)

            def rows_in_regions(k, g, place):
                dve.wait_ge(px_used, k + 1)
                for i in range(TG):
                    step(dve.tensor_tensor(BT[:, i + 1, :], PX[:, TG + i, :], BT[:, i, :], ALU.add))
                step(dve.tensor_tensor(POSM[:, :, :], PX[:, 0:TG, :], BT[:, 0:TG, :], ALU.add))
                step.later(dve.tensor_copy(BT[:, 0, :], BT[:, TG, :]))
                for c in range(TOPK):
                    step.later(dve.tensor_tensor(OHP[:, c, :, :], OH[:, c, tiles(g), :], POSM[:, :, :], ALU.mult))
                step.wait()
                step(dve.tensor_reduce(ROWF[:, :, :], OHP[:, :, :, :], AX_X, ALU.add))
                dve.tensor_scalar(IDX[:, place, :, :], ROWF[:, :, :], 0.0, None, ALU.add).then_inc(idx_ready, 1)

            def weigh(ph):
                dve.wait_ge(exp_ready, ph + 1)
                step(dve.tensor_tensor(OHD[:, :, :], OH[:, :, :, :].rearrange("p c t e -> p (c t) e"),
                                       PES[:, :].unsqueeze(1).broadcast_to([P, TOPK * T, E]), ALU.mult))
                step(dve.tensor_reduce(PK[:, :], OHD[:, :, :], AX_X, ALU.add))
                step(dve.tensor_scalar(WZ[:, :], EX[:, :], 1.0, None, ALU.add))
                step(dve.reciprocal(WZ[:, :], WZ[:, :]))
                step(dve.scalar_tensor_tensor(out=CW[:, :, 0], in0=PK[:, 0:T], scalar=0.5, in1=WZ[:, :],
                                              op0=ALU.mult, op1=ALU.mult))
                step(dve.tensor_tensor(WZ[:, :], WZ[:, :], EX[:, :], ALU.mult))
                step(dve.scalar_tensor_tensor(out=CW[:, :, 1], in0=PK[:, T:2 * T], scalar=0.5, in1=WZ[:, :],
                                              op0=ALU.mult, op1=ALU.mult))

            def table(ph):
                n = TG * GROUPS + 1
                step.wait()
                dve.tensor_copy(TAILI[:, :], BT[:, 0, :]).then_inc(tails_ready, 1)
                step(dve.tensor_tensor(CNT[:, :], BT[:, 0, :], REG0, ALU.subtract))
                cmp = CMP[:, :].rearrange("p (e k) -> p e k", k=n)
                step(dve.tensor_tensor(cmp, CNT[:, :].unsqueeze(2).broadcast_to([P, E, n]),
                                       KTH.rearrange("p (e k) -> p e k", k=n), ALU.is_gt))
                step(dve.tensor_reduce(NT[:, :], cmp, AX_X, ALU.add))
                tri = CMP[:, 0:E * E].rearrange("p (e f) -> p e f", f=E)
                step(dve.tensor_tensor(tri, NT[:, :].unsqueeze(1).broadcast_to([P, E, E]),
                                       TRI.rearrange("p (e f) -> p e f", f=E), ALU.mult))
                step(dve.tensor_reduce(END[:, :], tri, AX_X, ALU.add))
                slt = SLT[:, :].rearrange("p (s e) -> p s e", e=E)
                step(dve.tensor_tensor(slt, SIOTA.rearrange("p (s e) -> p s e", e=E),
                                       END[:, :].unsqueeze(1).broadcast_to([P, SLOTS, E]), ALU.is_ge))
                step(dve.tensor_reduce(EID[:, :], slt, AX_X, ALU.add))
                step(dve.tensor_tensor(slt, slt, NT[:, :].unsqueeze(1).broadcast_to([P, SLOTS, E]), ALU.mult))
                step(dve.tensor_reduce(ST0[:, :], slt, AX_X, ALU.add))
                step(dve.tensor_tensor(ST0[:, :], SROW, ST0[:, :], ALU.subtract))
                step(dve.tensor_scalar(ST0[:, :], ST0[:, :], float(P), None, ALU.mult))
                step(dve.scalar_tensor_tensor(out=ST0[:, :], in0=EID[:, :], scalar=float(REGION), in1=ST0[:, :],
                                              op0=ALU.mult, op1=ALU.add))
                step(dve.tensor_copy(ROWI[:, :], ST0[:, :]))
                step(dve.tensor_scalar(EID[:, :], EID[:, :], float(E - 1), float(EW), ALU.min, ALU.mult))
                dve.tensor_copy(WOFI[:, :], EID[:, :]).then_inc(table_ready, 1)
                dve.wait_ge(tails_ready, ph + 1)
                step(dve.tensor_copy(BT[:, 0, :], REG0))
            def ffn(ph):
                b = SLOTS * ph

                def gate(s, r):
                    dve.wait_ge(gelu_done, b + s + 1)
                    need(dve, at_done, b + s - 1)
                    dve.tensor_tensor(AV[r % 2][:, :], HPS[r % 2][:, HID:GW], GA[r % 2][:, :], ALU.mult)\
                        .then_inc(av_ready, 1)

                def result(s, r, i):
                    dve.wait_ge(y_done, b + s + 1)
                    need(dve, ys_out[r], 16 * (i + SLOTS // XRING * ph))
                    dve.tensor_copy(YO[:, r, :], YPS[r % 2]).then_inc(yo_ready, 1)

                def ffn_round(i):
                    for r in range(XRING):
                        s = i * XRING + r
                        if not (isinstance(s, int) and s + 2 >= SLOTS):
                            gate(s + 2, r)
                        result(s, r, i)

                gate(0, 0)
                gate(1, 1)
                ffn_round(0)
                with dve.Fori(1, SLOTS // XRING - 1) as i:
                    ffn_round(i)
                ffn_round(SLOTS // XRING - 1)

            def combine(g, place, loads):
                dve.wait_ge(yg_in[place], 16 * TOPK * loads)
                for c in range(TOPK):
                    for i in range(TG):
                        xt = X[:, g * TG + i, :]
                        last = c == TOPK - 1 and i == TG - 1
                        if i == 0 or last:
                            step.wait()
                        dve.scalar_tensor_tensor(out=xt, in0=YG[place][:, c, i, :], scalar=CW[:, g * TG + i, c:c + 1],
                                                 in1=xt, op0=ALU.mult, op1=ALU.add)\
                            .then_inc(yg_used if last else dve_step, 1)
                        step.n += not last

            def attend(g, j):
                k = g * UNITS + j

                def of(lag):
                    return unit_on(k - lag)

                kr = GROUPS + g - 2
                last = isinstance(g, int) and g == GROUPS + 1
                if on(g + 1) and j == 1:
                    dve.wait_ge(yg_used, g + 2)
                if on(g - 2) and j == 3:
                    dve.wait_ge(lg_used, kr + 1)
                c = j % C
                keys = slice(W if c == 0 else 0, 2 * W)
                n, m = (W if c == 0 else 2 * W), NP - BIASED
                if of(0):
                    dve.wait_ge(s_done, k + 1)
                    need(dve, b_ready, k - 1)
                    step(dve.tensor_reduce(MX[j % 2][:, :], SPS[j % 2][:, :, keys], AX_X, ALU.max, negate=True))
                if of(4):
                    dve.wait_ge(r_done, k - 3)
                    o = OPS[:, 0:SIDES * P].rearrange("p (a v) -> p a v", v=SLOT)
                    step(dve.reciprocal(RD[:, :], o[:, :, 2 * DH]))
                    need(dve, ot_done, k - 5)
                    for h in range(2):
                        hp = slice(h * W, (h + 1) * W)
                        dve.tensor_tensor(OS[hp, j % 2, h, :, :], o[hp, :, h * DH:(h + 1) * DH],
                                          RD[hp, :].unsqueeze(2).broadcast_to([W, NP, DH]), ALU.mult).then_inc(o_ready, 1)
                if j % C == 2:
                    s, par = stage_sequence(g, j - 1)
                    if seq_on(s):
                        dve.wait_ge(v_done, s + 1)
                        need(dve, pv_done, (s - 1) * C)
                        dve.tensor_tensor(V[:, par * C:(par + 1) * C, :, 0:2 * DH],
                                          M1.rearrange("p (w a v) -> p w a v", w=C, a=NP),
                                          BV[:, :].rearrange("p (a v) -> p a v", a=NP).unsqueeze(1)
                                          .broadcast_to([P, C, NP, 2 * DH]), ALU.add).then_inc(v_ready, 1)
                if of(7) and j % 2 == 1:
                    t = g * TG + (j - 7) // 2
                    dve.wait_ge(pj_done, t + 1)
                    dve.tensor_tensor(X[:, t, :], PVP[:, 0:D], X[:, t, :], ALU.add).then_inc(res_done, 1)
                if on(g - 1) and j == 5:
                    dve.wait_ge(res_done, g * TG)
                if of(0):
                    need(dve, t_done, 2 * (k - C + 1))
                    dve.tensor_tensor(PR[c][:, 0:m, keys], SPS[j % 2][:, 0:m, keys],
                                      MX[j % 2][:, 0:m].unsqueeze(2).broadcast_to([P, m, n]), ALU.add)\
                        .then_inc(d_ready, 1)
                if on(g - 2) and j == 2:
                    scale_logits(kr, RT["stok"][:, :], M1)
                if on(g - 2) and j == 4:
                    take_prefixes(kr, M1)
                if on(g + 1):
                    if j == 0:
                        combine(g + 1, 0, g + 2)
                    if j == 1:
                        row_stats(g + 1, BST)
                        moments(LN, slice(0, TG)).then_inc(lnvar_ready, 1)
                    if j == 2:
                        attention_rows(g + 1)
                if on(g - 1) and j == 5:
                    row_stats(g - 1, BST)
                    moments(RT, slice(0, TG)).then_inc(var_ready, 1)
                if on(g - 2):
                    if j == 0:
                        dve.wait_ge(rstd_ready, PARTS + g - 1)
                        if not last:
                            dve.wait_ge(scattered, 16 * TG * TOPK * kr)
                        rows_of(kr, g - 2, 1 if last else 0, RT, lambda i: slice(i, i + 1))
                        dve.wait_ge(stok_ready, PARTS + g - 1)
                    if j == 3:
                        choose(kr, g - 2)
                    if j == 4:
                        rows_in_regions(kr, g - 2, 1 if last else 0)

            def attention_rows(g):
                dve.wait_ge(lnrstd_ready, g + 1)
                need(dve, xat_done, 2 * g)
                for i in range(TG):
                    if i == TG - 1:
                        step.wait()
                    ins = normalise(XA[:, i, :], g * TG + i, LN, slice(i, i + 1))
                    if i < TG - 1:
                        step.later(ins)
                ins.then_inc(xa_ready, 1)
                dve.wait_ge(xa_ready, g + 1)
                step(dve.tensor_tensor(X[:, tiles(g), :], X[:, tiles(g), :],
                                       BO[:, :].unsqueeze(1).broadcast_to([P, TG, D]), ALU.add))

            step.later(dve.memset(XAT[:, :, 0:W], 0.0))
            step.later(dve.memset(K[:, :, 0:W], 0.0))
            step.later(dve.memset(PR[0][:, :, 0:W], 0.0))
            step.later(dve.memset(OS[:, :, :, :, :], 0.0))
            step.later(dve.memset(V[:, :, :, 2 * DH:2 * DH + 1], 1.0))
            step.later(dve.memset(V[:, :, :, 2 * DH + 1:SLOT], 0.0))
            def part_stats(h):
                dve.wait_ge(x_loaded[h], 16)
                tiles_of_part = part_tiles(h)
                for i in range(T // PARTS):
                    step.later(dve.bn_stats(BST[:, i, :], X[:, tiles_of_part.start + i, :]))
                moments(ALL, tiles_of_part).then_inc(var_ready, 1)

            def first_rows(k):
                dve.wait_ge(rstd_ready, k * PARTS // GROUPS + 1)
                rows_of(k, k, k, ALL, lambda i: slice(k * TG + i, k * TG + i + 1))

            def first_route(k):
                dve.wait_ge(stok_ready, k * PARTS // GROUPS + 1)
                scale_logits(k, ALL["stok"][:, tiles(k)], ROUTER[0][1])
                dve.wait_ge(lg_used, k + 1)
                if k + 2 < GROUPS:
                    first_rows(k + 2)
                choose(k, k)
                take_prefixes(k, ROUTER[0][2])
                rows_in_regions(k, k, k)

            part_stats(0)
            dve.wait_ge(w_loaded, 16 * WEIGHT_LOADS)
            step(dve.tensor_copy(BT[:, 0, :], REG0))
            dve.wait_ge(pool_consts, 1)
            dve.tensor_copy(FILL[:, :, D].bitcast(U32), FROW).then_inc(fill_ready, 1)
            dve.tensor_scalar(RWS[:, :], RW[:, :], RS[:, :], float(D) ** -0.5, ALU.mult, ALU.mult).then_inc(consts_set, 1)
            part_stats(1)
            first_rows(0)
            first_rows(1)
            for k in range(GROUPS):
                first_route(k)
                if k % 2 == 0 and k // 2 + 2 < PARTS:
                    part_stats(k // 2 + 2)
            table(0)
            ffn(0)
            weigh(0)
            for g in range(-1, 2):
                for j in range(UNITS):
                    attend(g, j)
            with dve.Fori(2, GROUPS - 1) as g:
                step.enter(g, 2, STEPS_GROUP)
                for j in range(UNITS):
                    attend(g, j)
                step.leave(GROUPS - 3)
            for g in range(GROUPS - 1, GROUPS + 2):
                for j in range(UNITS):
                    attend(g, j)
            table(1)
            ffn(1)
            weigh(1)
            with dve.Fori(0, GROUPS // 2) as i:
                step.enter(i, 0, 2 * (TOPK * TG - 1))
                for par in range(2):
                    combine(i * 2 + par, par, i + 1 + (GROUPS if par == 0 else 0))
                step.leave(GROUPS // 2)


STEPS_GROUP = 69


def kernel(L0_attn_x, L0_attn_Wq, L0_attn_bq, L0_attn_Wk, L0_attn_bk, L0_attn_Wv, L0_attn_bv, L0_attn_Wo,
           L0_attn_bo, L0_ffn_router_scale, L0_ffn_router_w, L0_ffn_gating_w, L0_ffn_linear_w,
           L0_ffn_per_expert_scale):
    import numpy as np
    import concourse.bacc as bacc
    from concourse.bass_utils import run_bass_kernel_spmd

    def rows(v):
        return np.ascontiguousarray(np.broadcast_to(np.asarray(v)[None, :], (P, len(v))))

    pair_order = np.arange(D).reshape(2, NP, DH).transpose(1, 0, 2).reshape(-1)
    gates = np.asarray(L0_ffn_gating_w).transpose(3, 0, 1, 2).reshape(P, E, GW)
    linear = np.asarray(L0_ffn_linear_w).reshape(E, 2, P, D).transpose(2, 0, 1, 3).reshape(P, E, 2 * D)
    part, n_k = np.arange(P), TG * GROUPS + 1

    query_mask = (part % HALF)[:, None] // DH == np.arange(NP)[None, :]
    consts = np.concatenate([
        np.eye(P), part[:, None] < part[None, :], np.ones((P, P)), query_mask,
        np.tile(np.arange(E), (P, 1)), np.tile(np.arange(E) * REGION, (P, 1)),
        np.tile(np.arange(n_k) * P, (P, E)), np.tile(np.repeat(np.arange(SLOTS), E), (P, 1)),
        np.tile((np.arange(E)[None, :] <= np.arange(E)[:, None]).reshape(-1), (P, 1)),
        np.tile(np.arange(SLOTS), (P, 1)), part[:, None] + np.arange(T) * P,
        part[:, None] + TOPK * NSEQ * L + np.arange(FILLERS) * P], axis=1).astype(np.float32)
    arrays = dict(
        x=np.asarray(L0_attn_x).reshape(NSEQ * L, D),
        wq=np.asarray(L0_attn_Wq)[pair_order].T, bq=np.asarray(L0_attn_bq)[pair_order].reshape(P, 1),
        wk=np.asarray(L0_attn_Wk)[pair_order].T, bk=np.asarray(L0_attn_bk)[pair_order].reshape(P, 1),
        wv=np.asarray(L0_attn_Wv)[pair_order].T, bv=rows(np.asarray(L0_attn_bv)[pair_order]),
        wo=np.asarray(L0_attn_Wo).T, bo=rows(L0_attn_bo),
        rscale=np.asarray(L0_ffn_router_scale).reshape(P, 1), rw=np.asarray(L0_ffn_router_w),
        experts=np.concatenate([gates, linear], axis=2).reshape(P, E * EW),
        pes=rows(L0_ffn_per_expert_scale), consts=consts)
    arrays = {n: np.ascontiguousarray(a) for n, a in arrays.items()}
    nc = bacc.Bacc("TRN2", target_bir_lowering=False, num_devices=1)
    aps = {n: nc.dram_tensor(n, a.shape, F32, kind="ExternalInput").ap() for n, a in arrays.items()}
    out = nc.dram_tensor("out", (NSEQ * L, D), F32, kind="ExternalOutput").ap()
    macaron(nc, out=out, **aps)
    r = run_bass_kernel_spmd(nc, [arrays], core_ids=[0])
    return np.asarray(r.results[0]["out"]).reshape(NSEQ, L, D)
```

```python
from contextlib import ExitStack

import concourse.bass as bass
from concourse import mybir

F32 = mybir.dt.float32
I32 = mybir.dt.int32
U32 = mybir.dt.uint32
ALU = mybir.AluOpType
ACT = mybir.ActivationFunctionType
AX_X = mybir.AxisListType.X

P = 128
NSEQ, L, D = 16, 256, 128
T = NSEQ * L // P
TG = 4
GROUPS = T // TG
H, DH, W = 16, 8, 64
NP = H // 2
C = L // W
UNITS = TG * P // W
SLOT = 32
PAIRS, SIDES = P // SLOT, NP * SLOT // P
BIASED = 4
HALF = P // 2
HP = NP // 2
PADL = W + L
E, HID, TOPK = 8, 256, 2
GW = 2 * HID
EW = GW + 2 * D
REGION = NSEQ * L + P
RING = 4
XRING = 2 * RING
SLOTS = -(-((NSEQ * L * TOPK + E * (P - 1)) // P) // XRING) * XRING
SPARE = SLOTS - NSEQ * L * TOPK // P + 1
ROWS = E * REGION + SPARE * P
FILLERS = E + SPARE
PARTS = 4
STEPS_GROUP = 69
DIRECT = 2
BOUNDED = "computed on chip from counts that add up to the tokens"
SCALE = float(DH) ** -0.5
LN_EPS, RMS_EPS = 1e-5, 1e-6


def need(eng, sem, value):
    if not (isinstance(value, int) and value <= 0):
        eng.wait_ge(sem, value)


class Steps:

    def __init__(self, eng, sem):
        self.eng, self.sem, self.base, self.n = eng, sem, 0, 0

    def __call__(self, ins):
        self.n += 1
        ins.then_inc(self.sem, 1)
        self.eng.wait_ge(self.sem, self.base + self.n)

    def later(self, ins):
        self.n += 1
        ins.then_inc(self.sem, 1)

    def wait(self):
        self.eng.wait_ge(self.sem, self.base + self.n)

    def enter(self, index, first, per):
        self.outside = self.base + self.n
        self.base, self.n, self.per = self.outside + (index - first) * per, 0, per

    def leave(self, times):
        assert self.n == self.per, f"steps in the body: {self.n}, not {self.per}"
        self.base, self.n = self.outside + times * self.per, 0


def macaron(nc, x, wq, bq, wk, bk, wv, bv, wo, bo, rscale, rw, experts, pes, consts, out):
    xs = nc.dram_tensor("xs_rows", [ROWS, D + 1], F32, kind="Internal").ap()
    ys = nc.dram_tensor("ys_rows", [TOPK * NSEQ * L + FILLERS * P, D], F32, kind="Internal").ap()
    x_tiles = x.rearrange("(t p) d -> p t d", p=P)
    out_tiles = out.rearrange("(t p) d -> p t d", p=P)
    ys_tiles = ys[0:TOPK * NSEQ * L, :].rearrange("(c t p) d -> p c t d", c=TOPK, p=P)

    with ExitStack() as ctx:
        def sb(name, shape, dt=F32):
            return ctx.enter_context(nc.sbuf_tensor(name, shape, dt))

        def sem(name):
            return ctx.enter_context(nc.semaphore(name))

        X = sb("X", [P, T, D])
        EXP = sb("EXP", [P, E * EW])
        WQ, WK, WV, WO = [sb(name, [P, D]) for name in ("WQ", "WK", "WV", "WO")]
        BQ, BK = sb("BQ", [P, 1]), sb("BK", [P, 1])
        BQS, TINY = sb("BQS", [P, 1]), sb("TINY", [P, 1])
        BV, BO = sb("BV", [P, D]), sb("BO", [P, D])
        RS, RW, RWS = sb("RS", [P, 1]), sb("RW", [P, E]), sb("RWS", [P, E])
        PES = sb("PES", [P, E])
        CN = sb("CN", [P, consts.shape[1]])
        o = 0
        parts = []
        for n in (P, P, P, NP, E, E, E * (TG * GROUPS + 1), SLOTS * E, E * E, SLOTS, T, FILLERS):
            parts.append(CN[:, o:o + n])
            o += n
        IDN, BEFORE, ONES, QMASK, IOTA, REG0, KTH, SIOTA, TRI, SROW, TOKEN, FROW = parts
        Q = sb("Q", [P, 2, C, HP, 2, W])
        K = sb("K", [P, 2, PADL])
        QS = sb("QS", [P, L])
        V = sb("V", [P, 2 * C, NP, SLOT])
        CW = sb("CW", [P, T, TOPK])
        NHALF, REPS, EULER = sb("NHALF", [P, T]), sb("REPS", [P, T]), sb("EULER", [P, T])
        FILL = sb("FILL", [P, FILLERS, D + 1])
        ALL, LN, RT = [{m: sb(f"{m}_{which}", [P, n]) for m in ("mean", "var", "vareps", "rstd", "msq", "stok")}
                       for which, n in (("all", T), ("ln", TG), ("rt", TG))]
        BST = sb("BST", [P, T // PARTS, 6])
        MSUM, MDIF, M2S = [sb(name, [P, T // PARTS]) for name in ("MSUM", "MDIF", "M2S")]
        XN = sb("XN", [P, TOPK, GROUPS, TG, D + 1])
        XNT = sb("XNT", [P, TG * P])
        LGS, TOP = sb("LGS", [P, TG, E]), sb("TOP", [P, TG, E])
        TIX, IXF = sb("TIX", [P, TG, E], U32), sb("IXF", [P, TOPK, TG])
        OH = sb("OH", [P, TOPK, T, E])
        IND = sb("IND", [P, TG, E])
        DL, EX, WZ = sb("DL", [P, T]), sb("EX", [P, T]), sb("WZ", [P, T])
        OHP, PK = sb("OHP", [P, TOPK, TG, E]), sb("PK", [P, TOPK * T])
        BT = sb("BT", [P, TG + 1, E])
        PX = sb("PX", [P, 2 * TG, E])
        POSM = sb("POSM", [P, TG, E])
        OHD = sb("OHD", [P, TOPK * T, E])
        ROWF = sb("ROWF", [P, TOPK, TG])
        IDX = sb("IDX", [P, GROUPS, TOPK, TG], U32)
        YG = sb("YG", [P, TOPK, TG, D])
        CNT, NT, END = sb("CNT", [P, E]), sb("NT", [P, E]), sb("END", [P, E])
        CMP = sb("CMP", [P, E * (TG * GROUPS + 1)])
        SLT = sb("SLT", [P, SLOTS * E])
        EID, ST0 = sb("EID", [P, SLOTS]), sb("ST0", [P, SLOTS])
        ROWI, WOFI, TAILI = sb("ROWI", [P, SLOTS], I32), sb("WOFI", [P, SLOTS], I32), sb("TAILI", [P, E], I32)
        XS = sb("XS", [P, XRING, D + 1])
        XST = [sb(f"XST{i}", [P, P]) for i in range(2)]
        GA = [sb(f"GA{i}", [P, HID]) for i in range(2)]
        AV = [sb(f"AV{i}", [P, HID]) for i in range(2)]
        WG = [sb(f"WG{i}", [P, GW]) for i in range(2)]
        YO = sb("YO", [P, XRING, D])
        XA = sb("XA", [P, TG, D])
        XAT = sb("XAT", [P, 2, PADL])
        MX = [sb(f"MX{i}", [P, NP]) for i in range(2)]
        PR = [sb(f"PR{i}", [P, NP, 2 * W]) for i in range(C)]
        PT = [sb(f"PT{i}", [P, NP, P]) for i in range(2)]
        PVS = sb("PVS", [P, SIDES, P])
        RD = sb("RD", [P, NP])
        OS = sb("OS", [P, 2, 2, NP, DH])
        OT = sb("OT", [P, 2, W])

        PS = ctx.enter_context(nc.psum_tensor("PS", [P, 8, 512], F32))
        HPS = [PS[:, i, :] for i in range(2)]
        XTP = [PS[:, 2 + i, 0:P] for i in range(2)]
        YPS = [PS[:, 6 + i, 0:D] for i in range(2)]
        SPS = [PS[:, 2 * i:2 * i + 2, :].rearrange("p a (b k) -> p (a b) k", k=P) for i in range(2)]
        TPS = PS[:, 4, :].rearrange("p (b k) -> p b k", k=P)
        OPS, PVP, M1 = PS[:, 5, :], PS[:, 6, :], PS[:, 7, :]
        ROUTER = [PS[:, 4, :], PS[:, 5, :], PS[:, 6, :]]

        x_loaded = [sem(f"x_loaded{h}") for h in range(PARTS)]
        w_loaded, e_loaded, xs_zeroed = sem("w_loaded"), sem("e_loaded"), sem("xs_zeroed")
        consts_set = sem("consts_set")
        pool_consts = sem("pool_consts")
        dve_step, act_step, pool_step = sem("dve_step"), sem("act_step"), sem("pool_step")
        var_ready, rstd_ready, stok_ready = sem("var_ready"), sem("rstd_ready"), sem("stok_ready")
        diff_ready, exp_ready = sem("diff_ready"), sem("exp_ready")
        xn_ready, rt_done, xnt_ready = sem("xn_ready"), sem("rt_done"), sem("xnt_ready")
        lg_done, ind_ready, px_done = sem("lg_done"), sem("ind_ready"), sem("px_done")
        lg_used, px_used = sem("lg_used"), sem("px_used")
        idx_ready = sem("idx_ready")
        scattered = sem("scattered")
        tails_ready = sem("tails_ready")
        table_ready, tails_zeroed = sem("table_ready"), sem("tails_zeroed")
        xs_in = [sem(f"xs_in{i}") for i in range(XRING)]
        ys_out = [sem(f"ys_out{i}") for i in range(XRING)]
        xt_done, xst_ready, h_done = sem("xt_done"), sem("xst_ready"), sem("h_done")
        gelu_done, av_ready, wg_ready = sem("gelu_done"), sem("av_ready"), sem("wg_ready")
        y_done, yo_ready = sem("y_done"), sem("yo_ready")
        yg_in, yg_used = sem("yg_in"), sem("yg_used")
        results_in, combined = [sem(f"results_in{g}") for g in range(GROUPS)], sem("combined")
        cw_ready, weighted = sem("cw_ready"), sem("weighted")
        fill_ready, xn2_ready = sem("fill_ready"), sem("xn2_ready")
        lnvar_ready, lnrstd_ready = sem("lnvar_ready"), sem("lnrstd_ready")
        xa_ready, xat_done, xat_ready = sem("xa_ready"), sem("xat_done"), sem("xat_ready")
        q_done, q_ready, k_done, k_ready = sem("q_done"), sem("q_ready"), sem("k_done"), sem("k_ready")
        v_done, v_ready = sem("v_done"), sem("v_ready")
        qm_ready, s_done, d_ready, p_ready = sem("qm_ready"), sem("s_done"), sem("d_ready"), sem("p_ready")
        b_ready = sem("b_ready")
        pvs_ready, r_done = sem("pvs_ready"), sem("r_done")
        t_done, pt_ready, pv_done, o_ready = sem("t_done"), sem("pt_ready"), sem("pv_done"), sem("o_ready")
        ot_done, ot_ready, pj_done, res_done = sem("ot_done"), sem("ot_ready"), sem("pj_done"), sem("res_done")
        stored, groups_sent, tiles_sent = sem("stored"), sem("groups_sent"), sem("tiles_sent")

        WEIGHT_LOADS = 12

        def tiles(g, n=TG):
            return bass.ds(g * TG, n)

        def on(g):
            return not isinstance(g, int) or 0 <= g < GROUPS

        def part_tiles(h):
            return slice(h * T // PARTS, (h + 1) * T // PARTS)

        def unit_on(k):
            return not isinstance(k, int) or 0 <= k < GROUPS * UNITS

        def seq_on(s):
            return not isinstance(s, int) or 0 <= s < NSEQ

        def stage_sequence(g, j):
            ahead = {0: 1, 1: 0, 2: 2, 3: 2}[j % C]
            s = 2 * g + j // C + ahead
            return s, (j // C + ahead) % 2

        def prefixes_step(g):
            return 5 if isinstance(g, int) and g == GROUPS else 4

        block = ctx.enter_context(nc.Block())

        @block.sync
        def _(sp):
            for h in range(PARTS):
                sp.dma_start(X[:, part_tiles(h), :], x_tiles[:, part_tiles(h), :]).then_inc(x_loaded[h], 16)
            for dst, src in ((CN, consts), (RS, rscale), (RW, rw), (PES, pes), (WQ, wq), (WK, wk), (WV, wv),
                             (BQ, bq), (BK, bk), (BV, bv), (BO, bo)):
                sp.dma_start(dst[:, :], src).then_inc(w_loaded, 16)
            sp.dma_start(WO[:, :], wo).then_inc(w_loaded, 16)
            sp.dma_start(EXP[:, :], experts).then_inc(e_loaded, 16)
            sp.wait_ge(fill_ready, 1)
            sp.dma_start(xs[E * REGION:ROWS, :].rearrange("(n p) d -> p n d", p=P), FILL[:, E:, :]).then_inc(xs_zeroed, 16)

            def row_at(reg, entry, high):
                sp.load(reg, entry)
                return nc.s_assert_within(sp.snap(reg), min_val=0, max_val=high, skip_runtime_bounds_check_because=BOUNDED)

            row_regs = [sp.alloc_register(f"row{r}") for r in range(XRING)]

            def ffn(ph):
                sp.wait_ge(tails_ready, ph + 1)
                for e in range(E):
                    r = row_at(row_regs[e], TAILI[0:1, e:e + 1], ROWS - P)
                    sp.dma_start(xs[bass.ds(r, P), :], FILL[:, e, :]).then_inc(tails_zeroed, 16)
                sp.wait_ge(table_ready, ph + 1)
                sp.wait_ge(tails_zeroed, 16 * E * (ph + 1))
                sp.wait_ge(xs_zeroed, 16)
                sp.wait_ge(scattered, 16 * TG * TOPK * GROUPS * (ph + 1))

                def load(i, r):
                    need(sp, ys_out[r], 16 * (i + SLOTS // XRING * ph))
                    row = row_at(row_regs[r], ROWI[0:1, bass.ds(i * XRING + r, 1)], ROWS - P)
                    sp.dma_start(XS[:, r, :], xs[bass.ds(row, P), :]).then_inc(xs_in[r], 16)

                for r in range(XRING):
                    load(0, r)
                with sp.Fori(1, SLOTS // XRING) as i:
                    for r in range(XRING):
                        load(i, r)
                for r in range(XRING):
                    sp.wait_ge(ys_out[r], 16 * (SLOTS // XRING) * (ph + 1))

            def load_results(g):
                for c in range(TOPK):
                    sp.dma_start(YG[:, c, :, :], ys_tiles[:, c, tiles(g), :]).then_inc(yg_in, 16)

            ffn(0)
            load_results(0)
            with sp.Fori(1, GROUPS) as g:
                sp.wait_ge(yg_used, g)
                load_results(g)
            ffn(1)
            for g in range(GROUPS):
                for c in range(TOPK):
                    sp.dma_start(XN[:, c, g, :, 0:D], ys_tiles[:, c, tiles(g), :]).then_inc(results_in[g], 16)
            with sp.Fori(0, GROUPS - 1) as g:
                sp.wait_ge(combined, (g + 1) * TG)
                sp.dma_start(out_tiles[:, tiles(g), :], X[:, tiles(g), :]).then_inc(stored, 16)
            for h in range(2):
                t = (GROUPS - 1) * TG + h * TG // 2
                sp.wait_ge(combined, t + TG // 2)
                sp.dma_start(out_tiles[:, t:t + TG // 2, :], X[:, t:t + TG // 2, :]).then_inc(stored, 16)
            sp.wait_ge(stored, 16 * (GROUPS + 1))

        @block.gpsimd
        def _(pool):
            pool.memset(FILL[:, :, :], 0.0).then_inc(pool_consts, 1)
            step = Steps(pool, pool_step)
            step.later(pool.memset(NHALF[:, :], -0.5))
            step.later(pool.memset(REPS[:, :], RMS_EPS))
            step(pool.memset(EULER[:, :], 2.718281828459045))

            def router_scales(st, at, done):
                rstd, msq, stok, n = st["rstd"][:, at], st["msq"][:, at], st["stok"][:, at], at.stop - at.start
                pool.tensor_tensor(rstd, st["vareps"][:, at], NHALF[:, 0:n], ALU.pow).then_inc(rstd_ready, 1)
                pool.wait_ge(rstd_ready, done + 1)
                step(pool.tensor_tensor(msq, rstd, rstd, ALU.mult))
                step(pool.tensor_tensor(msq, msq, st["var"][:, at], ALU.mult))
                step(pool.tensor_tensor(msq, msq, REPS[:, 0:n], ALU.add))
                pool.tensor_tensor(stok, msq, NHALF[:, 0:n], ALU.pow).then_inc(stok_ready, 1)

            def exponentials(ph):
                pool.wait_ge(diff_ready, GROUPS * (ph + 1))
                pool.tensor_tensor(EX[:, :], EULER[:, :], DL[:, :], ALU.pow).then_inc(exp_ready, 1)

            def route(k, place):
                pool.wait_ge(idx_ready, k + 1)
                pool.wait_ge(xn2_ready, k + 1)
                pool.sem_inc(groups_sent, 1)
                for i in range(TG):
                    for c in range(TOPK):
                        pool.indirect_dma_start(xs, bass.IndirectOffsetOnAxis(ap=IDX[:, place, c, i:i + 1], axis=0),
                                                XN[:, c, place, i, :], None).then_inc(scattered, 16)

            def results(ph):
                with pool.Fori(0, SLOTS // XRING) as i:
                    for r in range(XRING):
                        pool.wait_ge(yo_ready, SLOTS * ph + i * XRING + r + 1)
                        pool.sem_inc(tiles_sent, 1)
                        pool.indirect_dma_start(ys, bass.IndirectOffsetOnAxis(ap=XS[:, r, D:D + 1].bitcast(U32), axis=0),
                                                YO[:, r, :], None).then_inc(ys_out[r], 16)

            def part_scales(h):
                pool.wait_ge(var_ready, h + 1)
                router_scales(ALL, part_tiles(h), h)

            for h in range(PARTS):
                part_scales(h)
            for k in range(GROUPS):
                route(k, k)
            exponentials(0)

            def mask_queries(s, par):
                if seq_on(s):
                    pool.wait_ge(q_ready, s + 1)
                    need(pool, s_done, (s - 1) * C)
                    for c in range(C):
                        pool.tensor_tensor(Q[:, par, c, :, :, :].rearrange("p a h q -> p (a h) q"),
                                           QS[:, c * W:(c + 1) * W].unsqueeze(1).broadcast_to([P, NP, W]),
                                           QMASK.unsqueeze(2).broadcast_to([P, NP, W]), ALU.mult).then_inc(qm_ready, 1)

            def scales_of(g):
                pool.wait_ge(var_ready, PARTS + g)
                router_scales(RT, slice(0, TG), PARTS + g - 1)

            def body(g):
                mask_queries(2 * g + 1, 1)
                if on(g + 1):
                    pool.wait_ge(lnvar_ready, g + 2)
                    pool.tensor_tensor(LN["rstd"][:, :], LN["vareps"][:, :], NHALF[:, 0:TG], ALU.pow)\
                        .then_inc(lnrstd_ready, 1)
                mask_queries(2 * g + 2, 0)
                last_scales_first = isinstance(g, int) and g == GROUPS
                if last_scales_first:
                    scales_of(g)
                if on(g - 2):
                    route(GROUPS + g - 2, 1 if isinstance(g, int) and g == GROUPS + 1 else 0)
                if on(g - 1) and not last_scales_first:
                    scales_of(g)

            results(0)
            for g in range(-1, 2):
                body(g)
            with pool.Fori(2, GROUPS - 1) as g:
                step.enter(g, 2, 3)
                body(g)
                step.leave(GROUPS - 3)
            for g in range(GROUPS - 1, GROUPS + 2):
                body(g)
            exponentials(1)
            results(1)

        @block.tensor
        def _(pe):
            offsets = [pe.alloc_register(f"weight_offset{r}") for r in range(RING)]

            def transposes_of_router(k, place, bank):
                pe.wait_ge(xn_ready, TG * (k + 1))
                need(pe, xnt_ready, k)
                for i in range(TG):
                    ins = pe.transpose(bank[:, i * P:(i + 1) * P], XN[:, 0, place, i, 0:D], IDN)
                ins.then_inc(rt_done, 1)

            def logits(k, bank):
                need(pe, lg_used, k)
                pe.wait_ge(xnt_ready, k + 1)
                for i in range(TG):
                    ins = pe.matmul(bank[:, i * E:(i + 1) * E], XNT[:, i * P:(i + 1) * P], RWS[:, :],
                                    start=True, stop=True)
                ins.then_inc(lg_done, 1)

            def prefixes(k, bank):
                need(pe, px_used, k)
                pe.wait_ge(ind_ready, k + 1)
                ind = IND[:, :, :].rearrange("p t e -> p (t e)")
                pe.matmul(bank[:, 0:TG * E], BEFORE, ind, start=True, stop=True)
                pe.matmul(bank[:, TG * E:2 * TG * E], ONES, ind, start=True, stop=True).then_inc(px_done, 1)

            def ffn(ph):
                b = SLOTS * ph
                pe.wait_ge(table_ready, ph + 1)

                def transpose_in(s, r, rounds):
                    pe.wait_ge(xs_in[r], 16 * (rounds + 1 + SLOTS // XRING * ph))
                    pe.transpose(XTP[r % 2], XS[:, r, 0:D], IDN).then_inc(xt_done, 1)

                def load_offset(s, r):
                    pe.load(offsets[r % RING], WOFI[0:1, bass.ds(s, 1)])

                def gates(s, r):
                    pe.wait_ge(xst_ready, b + s + 1)
                    pe.wait_ge(wg_ready, b + s + 1)
                    for c in range(GW // P):
                        ins = pe.matmul(HPS[r % 2][:, c * P:(c + 1) * P], WG[r % 2][:, c * P:(c + 1) * P],
                                        XST[r % 2][:, :], start=True, stop=True)
                    ins.then_inc(h_done, 1)

                def down(s, r):
                    pe.wait_ge(av_ready, b + s + 1)
                    if isinstance(s, int) and s == SLOTS - 1:
                        pe.wait_ge(yo_ready, b + s - 1)
                    o = nc.s_assert_within(pe.snap(offsets[r % RING]), min_val=0, max_val=(E - 1) * EW,
                                           skip_runtime_bounds_check_because=BOUNDED)
                    for c in range(2):
                        ins = pe.matmul(YPS[r % 2], AV[r % 2][:, c * P:(c + 1) * P],
                                        EXP[:, bass.ds(o + (GW + c * D), D)], start=(c == 0), stop=(c == 1))
                    ins.then_inc(y_done, 1)

                def step(i, r):
                    s = i * XRING + r
                    last = isinstance(s, int) and s == SLOTS - 1
                    if not last:
                        transpose_in(s + 1, (r + 1) % XRING, i + (r + 1) // XRING)
                    gates(s, r)
                    if not (isinstance(s, int) and s == 0):
                        down(s - 1, (r - 1) % XRING)
                    load_offset(s, r)
                    if last:
                        down(s, r)

                transpose_in(0, 0, 0)
                for r in range(XRING):
                    step(0, r)
                with pe.Fori(1, SLOTS // XRING - 1) as i:
                    for r in range(XRING):
                        step(i, r)
                for r in range(XRING):
                    step(SLOTS // XRING - 1, r)

            def slot_a(g, j):
                s, par = stage_sequence(g, j)
                if not seq_on(s):
                    return
                if j % C == 2:
                    pe.wait_ge(xa_ready, g + 2)
                    need(pe, v_ready, s - 1)
                    if not seq_on(s - 2):
                        need(pe, k_ready, s)
                    if on(g - 2) and j == 2:
                        pe.wait_ge(lg_used, GROUPS + g - 1)
                    for i in range(L // P):
                        ins = pe.transpose(M1[:, i * P:(i + 1) * P], XA[:, par * 2 + i, :], IDN)
                    ins.then_inc(xat_done, 1)
                elif j % C == 1:
                    if seq_on(s + 1):
                        pe.wait_ge(k_ready, s + 2)
                    elif on(g - 2):
                        pe.wait_ge(px_used, GROUPS + g - 1)
                    if j == 1 and on(g - 2):
                        pe.wait_ge(xnt_ready, GROUPS + g - 1)
                    for c in range(C):
                        ins = pe.matmul(M1[:, c * P:(c + 1) * P], XAT[:, par, c * W:c * W + 2 * W], WV[:, :],
                                        start=True, stop=True)
                    ins.then_inc(v_done, 1)
                else:
                    if j % C == 3:
                        w, done = WQ, q_done
                        pe.wait_ge(xat_ready, s + 1)
                    else:
                        w, done = WK, k_done
                        pe.wait_ge(q_ready, s + 1)
                        if j == 4 and on(g - 2):
                            pe.wait_ge(px_used, GROUPS + g - 1)
                    pe.matmul(M1[:, 0:L], w[:, :], XAT[:, par, W:PADL], start=True, stop=True).then_inc(done, 1)

            def slot_b(g, j):
                k = GROUPS + g - 2
                if on(g - 2):
                    if j == 1:
                        if seq_on(2 * g + 1):
                            pe.wait_ge(k_ready, 2 * g + 2)
                        transposes_of_router(k, 1 if isinstance(g, int) and g == GROUPS + 1 else 0, M1)
                    if j == 2:
                        if seq_on(2 * g):
                            pe.wait_ge(v_ready, 2 * g + 1)
                        logits(k, M1)
                    if j == prefixes_step(g):
                        if seq_on(2 * g + 2):
                            pe.wait_ge(q_ready, 2 * g + 3)
                        prefixes(k, M1)

            def scores(g, j, half):
                c, par = j % C, j // C % 2
                first = 1 if c == 0 else 0
                rows = slice(half * HALF, (half + 1) * HALF)
                for p in range(HP):
                    ins = pe.matmul(SPS[j % 2][:, half * HP + p, first * W:2 * W], Q[rows, par, c, p, :, :],
                                    K[rows, par, (c + first) * W:(c + 2) * W], start=True, stop=True)
                return ins

            def attend(g, j):
                k = g * UNITS + j

                def of(lag):
                    return unit_on(k - lag)

                def transpose_probabilities(half):
                    for p in range(HP):
                        ins = pe.transpose(TPS[:, p, :], PR[(j - 2) % C][:, half * HP + p, :], IDN)
                    ins.then_inc(t_done, 1)

                if of(4):
                    pe.wait_ge(pvs_ready, k - 3)
                    if not of(6):
                        need(pe, o_ready, 2 * (k - 4))
                    for i in range(SIDES):
                        ins = pe.transpose(OPS[:, i * P:(i + 1) * P], PVS[:, i, :], IDN)
                    ins.then_inc(r_done, 1)
                if of(-1):
                    if (j + 1) % C == 0:
                        pe.wait_ge(k_ready, 2 * g + (j + 1) // C + 1)
                    if isinstance(k, int) and k + 1 < 2 * C:
                        pe.wait_ge(qm_ready, k + 2)
                    elif (j + 1) % C == 0:
                        pe.wait_ge(qm_ready, k + 1 + C)
                    need(pe, d_ready, k)
                    scores(g, j + 1, 0)
                if of(7) and j % 2 == 1:
                    if not of(4):
                        pe.wait_ge(ot_ready, k - 5)
                        pe.wait_ge(pvs_ready, GROUPS * UNITS)
                        pe.wait_ge(res_done, g * TG + (j - 7) // 2)
                    pe.matmul(PVP[:, 0:D], OT[:, :, :], WO[:, :], start=True, stop=True).then_inc(pj_done, 1)
                if of(2):
                    if not of(4):
                        pe.wait_ge(p_ready, k - 1)
                        need(pe, pt_ready, 2 * (k - 2))
                    transpose_probabilities(0)
                if of(-1):
                    need(pe, b_ready, k)
                    scores(g, j + 1, 1).then_inc(s_done, 1)
                if of(5):
                    if of(4):
                        pe.wait_ge(o_ready, 2 * (k - 3))
                    else:
                        pe.wait_ge(o_ready, 2 * (k - 4))
                        pe.wait_ge(ot_ready, k - 5)
                    pe.transpose(OPS[:, 0:P], OS[:, (j - 1) % 2, :, :, :].rearrange("p h a d -> p (h a d)"), IDN)\
                        .then_inc(ot_done, 1)
                slot_b(g, j)
                if of(2):
                    pe.wait_ge(pt_ready, 2 * (k - 2) + 1)
                    transpose_probabilities(1)
                if of(3):
                    if not of(2):
                        pe.wait_ge(pt_ready, 2 * (k - 2))
                    if (j - 3) % C == 0:
                        pe.wait_ge(v_ready, 2 * g + (j - 3) // C + 1)
                    if of(7) and j % 2 == 1:
                        pe.wait_ge(res_done, g * TG + (j - 7) // 2 + 1)
                    for p in range(NP):
                        i, rows = p // PAIRS, slice(p % PAIRS * SLOT, (p % PAIRS + 1) * SLOT)
                        ins = pe.matmul(PVP[rows, i * P:(i + 1) * P], V[:, (j - 3) % UNITS, p, :],
                                        PT[(j - 3) % 2][:, p, :], start=True, stop=True)
                    ins.then_inc(pv_done, 1)
                slot_a(g, j)

            pe.wait_ge(w_loaded, 16 * WEIGHT_LOADS)
            pe.wait_ge(consts_set, 1)
            rows_bank, logits_bank, prefixes_bank = ROUTER
            for k in range(GROUPS + 1):
                if k < GROUPS:
                    transposes_of_router(k, k, rows_bank)
                if k > 0:
                    prefixes(k - 1, prefixes_bank)
                if k < GROUPS:
                    logits(k, logits_bank)
            need(pe, px_used, GROUPS)
            pe.wait_ge(e_loaded, 16)
            ffn(0)
            pe.wait_ge(yo_ready, SLOTS)
            for g in range(-1, 2):
                for j in range(UNITS):
                    attend(g, j)
            with pe.Fori(2, GROUPS - 1) as g:
                for j in range(UNITS):
                    attend(g, j)
            for g in range(GROUPS - 1, GROUPS + 2):
                for j in range(UNITS):
                    attend(g, j)
            pe.wait_ge(px_used, 2 * GROUPS)
            ffn(1)

        @block.scalar
        def _(act):
            def router_rows(k, place, bank):
                act.wait_ge(rt_done, k + 1)
                need(act, lg_done, k)
                act.copy(XNT[:, :], bank).then_inc(xnt_ready, 1)
                act.copy(XN[:, 1, place, :, 0:D], XN[:, 0, place, :, 0:D]).then_inc(xn2_ready, 1)

            def ffn(ph):
                b = SLOTS * ph

                def rows(s, r):
                    act.wait_ge(xt_done, b + s + 1)
                    need(act, h_done, b + s - 1)
                    act.copy(XST[r % 2][:, :], XTP[r % 2]).then_inc(xst_ready, 1)

                def gelu(s, r):
                    act.wait_ge(h_done, b + s + 1)
                    need(act, av_ready, b + s - 1)
                    act.activation(GA[r % 2][:, :], HPS[r % 2][:, 0:HID], ACT.Gelu_apprx_tanh).then_inc(gelu_done, 1)

                def step(s, r):
                    if not (isinstance(s, int) and s == SLOTS - 1):
                        rows(s + 1, r + 1)
                    gelu(s, r)

                act.activation(TINY[:, :], BQ[:, :], ACT.Gelu_apprx_tanh).then_inc(act_step, 1)
                rows(0, 0)
                for s in range(RING):
                    step(s, s)
                with act.Fori(1, SLOTS // RING - 1) as i:
                    for r in range(RING):
                        step(i * RING + r, r)
                for s in range(SLOTS - RING, SLOTS):
                    step(s, s % RING)

            def evict_a(g, j):
                s, par = stage_sequence(g, j)
                if not seq_on(s):
                    return
                if j % C == 2:
                    act.wait_ge(xat_done, s + 1)
                    need(act, v_done, s - 1)
                    act.copy(XAT[:, par, W:PADL], M1[:, 0:L]).then_inc(xat_ready, 1)
                if j % C == 3:
                    act.wait_ge(q_done, s + 1)
                    need(act, qm_ready, s * C)
                    act.activation(QS[:, :], M1[:, 0:L], ACT.Identity, bias=BQS[:, :], scale=SCALE).then_inc(q_ready, 1)
                if j % C == 0:
                    act.wait_ge(k_done, s + 1)
                    need(act, s_done, (s - 1) * C)
                    act.activation(K[:, par, W:PADL], M1[:, 0:L], ACT.Identity, bias=BK[:, :]).then_inc(k_ready, 1)

            def attend(g, j):
                k = g * UNITS + j

                def of(lag):
                    return unit_on(k - lag)

                if of(1):
                    c = (j - 1) % C
                    keys = slice(W if c == 0 else 0, 2 * W)
                    act.wait_ge(d_ready, k)
                    for p in range(NP - BIASED, NP):
                        ins = act.activation(PR[c][:, p, keys], SPS[(j - 1) % 2][:, p, keys], ACT.Exp,
                                             bias=MX[(j - 1) % 2][:, p:p + 1])
                    ins.then_inc(b_ready, 1)
                evict_a(g if j > 0 else g - 1, (j - 1) % UNITS)
                if of(1):
                    pr = PR[c][:, 0:NP - BIASED, keys]
                    act.activation(pr, pr, ACT.Exp).then_inc(p_ready, 1)

                def probabilities(half):
                    act.wait_ge(t_done, 2 * (k - 2) + half + 1)
                    act.copy(PT[(j - 2) % 2][:, half * HP:(half + 1) * HP, :], TPS).then_inc(pt_ready, 1)

                if of(2):
                    probabilities(0)
                if of(5):
                    act.wait_ge(ot_done, k - 4)
                    for h in range(2):
                        hp = slice(h * W, (h + 1) * W)
                        ins = act.copy(OT[hp, (j - 5) % 2, :], OPS[hp, h * W:(h + 1) * W])
                    ins.then_inc(ot_ready, 1)
                if on(g - 2) and j == 1:
                    router_rows(GROUPS + g - 2, 1 if isinstance(g, int) and g == GROUPS + 1 else 0, M1)
                if of(2):
                    probabilities(1)
                if of(3):
                    act.wait_ge(pv_done, k - 2)
                    act.copy(PVS[:, :, :], PVP[:, 0:SIDES * P].rearrange("p (i t) -> p i t", i=SIDES))\
                        .then_inc(pvs_ready, 1)

            act.wait_ge(w_loaded, 16 * WEIGHT_LOADS)
            act.mul(BQS[:, :], BQ[:, :], SCALE).then_inc(act_step, 1)
            act.wait_ge(act_step, 1)
            router_rows(0, 0, ROUTER[0])
            with act.Fori(1, GROUPS) as k:
                router_rows(k, k, ROUTER[0])
            ffn(0)
            act.wait_ge(act_step, 2)
            act.activation(TINY[:, :], BQ[:, :], ACT.Exp).then_inc(act_step, 1)
            act.wait_ge(act_step, 3)
            for g in range(-1, 2):
                for j in range(UNITS):
                    attend(g, j)
            with act.Fori(2, GROUPS - 1) as g:
                for j in range(UNITS):
                    attend(g, j)
            for g in range(GROUPS - 1, GROUPS + 2):
                for j in range(UNITS):
                    attend(g, j)
            ffn(1)
            act.wait_ge(cw_ready, 1)
            for g in range(DIRECT, GROUPS):
                act.wait_ge(results_in[g], 16 * TOPK)
                for i in range(TG):
                    act.mul(XN[:, 0, g, i, 0:D], XN[:, 0, g, i, 0:D], CW[:, g * TG + i, 0:1]).then_inc(weighted, 1)

        @block.vector
        def _(dve):
            step = Steps(dve, dve_step)
            offsets = [dve.alloc_register(f"columns_offset{r}") for r in range(RING)]

            def row_stats(g, bst):
                for i in range(TG):
                    step.later(dve.bn_stats(bst[:, i, :], X[:, g * TG + i, :]))

            def moments(st, at):
                n = at.stop - at.start
                m0, q0, m1, q1 = (BST[:, 0:n, i] for i in (1, 2, 4, 5))
                step.wait()
                step.later(dve.tensor_tensor(MSUM[:, 0:n], m0, m1, ALU.add))
                step.later(dve.tensor_tensor(MDIF[:, 0:n], m0, m1, ALU.subtract))
                step(dve.tensor_tensor(M2S[:, 0:n], q0, q1, ALU.add))
                step.later(dve.tensor_scalar(st["mean"][:, at], MSUM[:, 0:n], 0.5, None, ALU.mult))
                step(dve.scalar_tensor_tensor(out=MDIF[:, 0:n], in0=MDIF[:, 0:n], scalar=0.25, in1=MDIF[:, 0:n],
                                              op0=ALU.mult, op1=ALU.mult))
                step(dve.scalar_tensor_tensor(out=st["var"][:, at], in0=M2S[:, 0:n], scalar=1.0 / D, in1=MDIF[:, 0:n],
                                              op0=ALU.mult, op1=ALU.add))
                return dve.tensor_scalar(st["vareps"][:, at], st["var"][:, at], LN_EPS, None, ALU.add)

            def rows_of(k, g, place, st, column):
                for c in range(TOPK):
                    step.later(dve.tensor_scalar(XN[:, c, place, :, D].bitcast(U32), TOKEN[:, tiles(g)],
                                                 float(c * NSEQ * L), None, ALU.add))
                for i in range(TG):
                    normalise(XN[:, 0, place, i, 0:D], g * TG + i, st, column(i)).then_inc(xn_ready, 1)

            def normalise(dst, t, st, a):
                return dve.tensor_scalar(dst, X[:, t, :], st["mean"][:, a], st["rstd"][:, a],
                                         ALU.subtract, ALU.mult)

            def scale_logits(k, stok, bank):
                dve.wait_ge(lg_done, k + 1)
                dve.tensor_tensor(LGS[:, :, :], bank[:, 0:TG * E].rearrange("p (t e) -> p t e", e=E),
                                  stok.unsqueeze(2).broadcast_to([P, TG, E]), ALU.mult).then_inc(lg_used, 1)

            def choose(k, g):
                for i in range(TG):
                    step.later(dve.max(TOP[:, i, :], LGS[:, i, :]))
                step.wait()
                dve.tensor_tensor(DL[:, tiles(g)], TOP[:, :, 1], TOP[:, :, 0], ALU.subtract).then_inc(diff_ready, 1)
                for i in range(TG):
                    step.later(dve.max_index(TIX[:, i, :], TOP[:, i, :], LGS[:, i, :]))
                step.wait()
                step(dve.tensor_copy(IXF[:, :, :], TIX[:, :, 0:TOPK].rearrange("p t c -> p c t")))
                for c in range(TOPK):
                    step.later(dve.tensor_tensor(OH[:, c, tiles(g), :], IOTA.unsqueeze(1).broadcast_to([P, TG, E]),
                                                 IXF[:, c, :].unsqueeze(2).broadcast_to([P, TG, E]), ALU.is_equal))
                step.wait()
                dve.tensor_tensor(IND[:, :, :], OH[:, 0, tiles(g), :], OH[:, 1, tiles(g), :], ALU.add).then_inc(ind_ready, 1)

            def take_prefixes(k, bank):
                dve.wait_ge(px_done, k + 1)
                dve.tensor_copy(PX[:, :, :], bank[:, 0:2 * TG * E].rearrange("p (t e) -> p t e", e=E)).then_inc(px_used, 1)

            def rows_in_regions(k, g, place):
                dve.wait_ge(px_used, k + 1)
                for i in range(TG):
                    step(dve.tensor_tensor(BT[:, i + 1, :], PX[:, TG + i, :], BT[:, i, :], ALU.add))
                step(dve.tensor_tensor(POSM[:, :, :], PX[:, 0:TG, :], BT[:, 0:TG, :], ALU.add))
                step.later(dve.tensor_copy(BT[:, 0, :], BT[:, TG, :]))
                for c in range(TOPK):
                    step.later(dve.tensor_tensor(OHP[:, c, :, :], OH[:, c, tiles(g), :], POSM[:, :, :], ALU.mult))
                step.wait()
                step(dve.tensor_reduce(ROWF[:, :, :], OHP[:, :, :, :], AX_X, ALU.add))
                dve.tensor_scalar(IDX[:, place, :, :], ROWF[:, :, :], 0.0, None, ALU.add).then_inc(idx_ready, 1)

            def weigh(ph):
                dve.wait_ge(exp_ready, ph + 1)
                step(dve.tensor_tensor(OHD[:, :, :], OH[:, :, :, :].rearrange("p c t e -> p (c t) e"),
                                       PES[:, :].unsqueeze(1).broadcast_to([P, TOPK * T, E]), ALU.mult))
                step(dve.tensor_reduce(PK[:, :], OHD[:, :, :], AX_X, ALU.add))
                step(dve.tensor_scalar(WZ[:, :], EX[:, :], 1.0, None, ALU.add))
                step(dve.reciprocal(WZ[:, :], WZ[:, :]))
                step(dve.scalar_tensor_tensor(out=CW[:, :, 0], in0=PK[:, 0:T], scalar=0.5, in1=WZ[:, :],
                                              op0=ALU.mult, op1=ALU.mult))
                step(dve.tensor_tensor(WZ[:, :], WZ[:, :], EX[:, :], ALU.mult))
                step(dve.scalar_tensor_tensor(out=CW[:, :, 1], in0=PK[:, T:2 * T], scalar=0.5, in1=WZ[:, :],
                                              op0=ALU.mult, op1=ALU.mult))

            def table(ph):
                n = TG * GROUPS + 1
                step.wait()
                dve.tensor_copy(TAILI[:, :], BT[:, 0, :]).then_inc(tails_ready, 1)
                step(dve.tensor_tensor(CNT[:, :], BT[:, 0, :], REG0, ALU.subtract))
                cmp = CMP[:, :].rearrange("p (e k) -> p e k", k=n)
                step(dve.tensor_tensor(cmp, CNT[:, :].unsqueeze(2).broadcast_to([P, E, n]),
                                       KTH.rearrange("p (e k) -> p e k", k=n), ALU.is_gt))
                step(dve.tensor_reduce(NT[:, :], cmp, AX_X, ALU.add))
                tri = CMP[:, 0:E * E].rearrange("p (e f) -> p e f", f=E)
                step(dve.tensor_tensor(tri, NT[:, :].unsqueeze(1).broadcast_to([P, E, E]),
                                       TRI.rearrange("p (e f) -> p e f", f=E), ALU.mult))
                step(dve.tensor_reduce(END[:, :], tri, AX_X, ALU.add))
                slt = SLT[:, :].rearrange("p (s e) -> p s e", e=E)
                step(dve.tensor_tensor(slt, SIOTA.rearrange("p (s e) -> p s e", e=E),
                                       END[:, :].unsqueeze(1).broadcast_to([P, SLOTS, E]), ALU.is_ge))
                step(dve.tensor_reduce(EID[:, :], slt, AX_X, ALU.add))
                step(dve.tensor_tensor(slt, slt, NT[:, :].unsqueeze(1).broadcast_to([P, SLOTS, E]), ALU.mult))
                step(dve.tensor_reduce(ST0[:, :], slt, AX_X, ALU.add))
                step(dve.tensor_tensor(ST0[:, :], SROW, ST0[:, :], ALU.subtract))
                step(dve.tensor_scalar(ST0[:, :], ST0[:, :], float(P), None, ALU.mult))
                step(dve.scalar_tensor_tensor(out=ST0[:, :], in0=EID[:, :], scalar=float(REGION), in1=ST0[:, :],
                                              op0=ALU.mult, op1=ALU.add))
                step(dve.tensor_copy(ROWI[:, :], ST0[:, :]))
                step(dve.tensor_scalar(EID[:, :], EID[:, :], float(E - 1), float(EW), ALU.min, ALU.mult))
                dve.tensor_copy(WOFI[:, :], EID[:, :]).then_inc(table_ready, 1)
                dve.wait_ge(tails_ready, ph + 1)
                step(dve.tensor_copy(BT[:, 0, :], REG0))

            def ffn(ph):
                b = SLOTS * ph

                def gate(s, r):
                    dve.wait_ge(gelu_done, b + s + 1)
                    need(dve, y_done, b + s - 1)
                    dve.tensor_tensor(AV[r % 2][:, :], HPS[r % 2][:, HID:GW], GA[r % 2][:, :], ALU.mult)\
                        .then_inc(av_ready, 1)

                def gate_columns(s, r):
                    dve.load(offsets[r % RING], WOFI[0:1, bass.ds(s, 1)])
                    o = nc.s_assert_within(dve.snap(offsets[r % RING]), min_val=0, max_val=(E - 1) * EW,
                                           skip_runtime_bounds_check_because=BOUNDED)
                    dve.tensor_copy(WG[r % 2][:, :], EXP[:, bass.ds(o, GW)]).then_inc(wg_ready, 1)

                def result(s, r, i):
                    dve.wait_ge(y_done, b + s + 1)
                    need(dve, ys_out[r], 16 * (i + SLOTS // XRING * ph))
                    dve.tensor_copy(YO[:, r, :], YPS[r % 2]).then_inc(yo_ready, 1)

                def ffn_round(i):
                    for r in range(XRING):
                        s = i * XRING + r
                        fixed = isinstance(s, int)
                        if not (fixed and s + 1 >= SLOTS):
                            gate(s + 1, r + 1)
                        result(s, r, i)
                        if not (fixed and s + 3 >= SLOTS):
                            gate_columns(s + 3, r + 3)

                dve.wait_ge(table_ready, ph + 1)
                dve.wait_ge(e_loaded, 16)
                gate_columns(0, 0)
                gate_columns(1, 1)
                gate(0, 0)
                gate_columns(2, 2)
                ffn_round(0)
                with dve.Fori(1, SLOTS // XRING - 1) as i:
                    ffn_round(i)
                ffn_round(SLOTS // XRING - 1)

            def combine(g):
                dve.wait_ge(yg_in, 16 * TOPK * (g + 1))
                for c in range(TOPK):
                    for i in range(TG):
                        last = c == TOPK - 1 and i == TG - 1
                        if i == 0 or last:
                            step.wait()
                        weighted_sum(g * TG + i, YG[:, c, i, :], c).then_inc(yg_used if last else dve_step, 1)
                        step.n += not last

            def weighted_sum(t, y, c):
                return dve.scalar_tensor_tensor(out=X[:, t, :], in0=y, scalar=CW[:, t, c:c + 1], in1=X[:, t, :],
                                                op0=ALU.mult, op1=ALU.add)

            def combine_last():
                def first_sums(g):
                    dve.wait_ge(results_in[g], 16 * TOPK)
                    if g >= DIRECT:
                        dve.wait_ge(weighted, (g - DIRECT + 1) * TG)
                        step.later(dve.tensor_tensor(X[:, tiles(g), :], X[:, tiles(g), :], XN[:, 0, g, :, 0:D], ALU.add))
                        return
                    for i in range(TG):
                        step.later(weighted_sum(g * TG + i, XN[:, 0, g, i, 0:D], 0))

                first_sums(0)
                for g in range(GROUPS):
                    first_done = step.base + step.n
                    if g + 1 < GROUPS:
                        first_sums(g + 1)
                    dve.wait_ge(dve_step, first_done)
                    for i in range(TG):
                        weighted_sum(g * TG + i, XN[:, 1, g, i, 0:D], 1).then_inc(combined, 1)

            def attend(g, j):
                k = g * UNITS + j

                def of(lag):
                    return unit_on(k - lag)

                kr = GROUPS + g - 2
                last = isinstance(g, int) and g == GROUPS + 1
                if on(g + 1) and j == 1:
                    dve.wait_ge(yg_used, g + 2)
                if on(g - 2) and j == 3:
                    dve.wait_ge(lg_used, kr + 1)
                c = j % C
                keys = slice(W if c == 0 else 0, 2 * W)
                n, m = (W if c == 0 else 2 * W), NP - BIASED
                if of(0):
                    dve.wait_ge(s_done, k + 1)
                    step(dve.tensor_reduce(MX[j % 2][:, :], SPS[j % 2][:, :, keys], AX_X, ALU.max, negate=True))
                if of(4):
                    dve.wait_ge(r_done, k - 3)
                    o = OPS[:, 0:SIDES * P].rearrange("p (a v) -> p a v", v=SLOT)
                    step(dve.reciprocal(RD[:, :], o[:, :, 2 * DH]))
                    for h in range(2):
                        hp = slice(h * W, (h + 1) * W)
                        dve.tensor_tensor(OS[hp, j % 2, h, :, :], o[hp, :, h * DH:(h + 1) * DH],
                                          RD[hp, :].unsqueeze(2).broadcast_to([W, NP, DH]), ALU.mult).then_inc(o_ready, 1)
                if j % C == 2:
                    s, par = stage_sequence(g, j - 1)
                    if seq_on(s):
                        dve.wait_ge(v_done, s + 1)
                        dve.tensor_tensor(V[:, par * C:(par + 1) * C, :, 0:2 * DH],
                                          M1.rearrange("p (w a v) -> p w a v", w=C, a=NP),
                                          BV[:, :].rearrange("p (a v) -> p a v", a=NP).unsqueeze(1)
                                          .broadcast_to([P, C, NP, 2 * DH]), ALU.add).then_inc(v_ready, 1)
                if of(7) and j % 2 == 1:
                    t = g * TG + (j - 7) // 2
                    dve.wait_ge(pj_done, t + 1)
                    dve.tensor_tensor(X[:, t, :], PVP[:, 0:D], X[:, t, :], ALU.add).then_inc(res_done, 1)
                if on(g - 1) and j == 5:
                    dve.wait_ge(res_done, g * TG)
                if of(0):
                    dve.tensor_tensor(PR[c][:, 0:m, keys], SPS[j % 2][:, 0:m, keys],
                                      MX[j % 2][:, 0:m].unsqueeze(2).broadcast_to([P, m, n]), ALU.add)\
                        .then_inc(d_ready, 1)
                if on(g - 2) and j == 2:
                    scale_logits(kr, RT["stok"][:, :], M1)
                if on(g - 2) and j == prefixes_step(g) == 4:
                    take_prefixes(kr, M1)
                if on(g + 1):
                    if j == 0:
                        combine(g + 1)
                    if j == 1:
                        row_stats(g + 1, BST)
                        moments(LN, slice(0, TG)).then_inc(lnvar_ready, 1)
                    if j == 2:
                        attention_rows(g + 1)
                if on(g - 1) and j == 5:
                    row_stats(g - 1, BST)
                    moments(RT, slice(0, TG)).then_inc(var_ready, 1)
                if on(g - 2) and j == prefixes_step(g) == 5:
                    take_prefixes(kr, M1)
                if on(g - 2):
                    if j == 0:
                        dve.wait_ge(rstd_ready, PARTS + g - 1)
                        if not last:
                            dve.wait_ge(scattered, 16 * TG * TOPK * kr)
                        rows_of(kr, g - 2, 1 if last else 0, RT, lambda i: slice(i, i + 1))
                        dve.wait_ge(stok_ready, PARTS + g - 1)
                    if j == 3:
                        choose(kr, g - 2)
                    if j == prefixes_step(g):
                        rows_in_regions(kr, g - 2, 1 if last else 0)

            def attention_rows(g):
                dve.wait_ge(lnrstd_ready, g + 1)
                need(dve, xat_done, 2 * g)
                for i in range(TG):
                    if i == TG - 1:
                        step.wait()
                    ins = normalise(XA[:, i, :], g * TG + i, LN, slice(i, i + 1))
                    if i < TG - 1:
                        step.later(ins)
                ins.then_inc(xa_ready, 1)
                dve.wait_ge(xa_ready, g + 1)
                step(dve.tensor_tensor(X[:, tiles(g), :], X[:, tiles(g), :],
                                       BO[:, :].unsqueeze(1).broadcast_to([P, TG, D]), ALU.add))

            step.later(dve.memset(XAT[:, :, 0:W], 0.0))
            step.later(dve.memset(K[:, :, 0:W], 0.0))
            step.later(dve.memset(PR[0][:, :, 0:W], 0.0))
            step.later(dve.memset(OS[:, :, :, :, :], 0.0))
            step.later(dve.memset(V[:, :, :, 2 * DH:2 * DH + 1], 1.0))
            step.later(dve.memset(V[:, :, :, 2 * DH + 1:SLOT], 0.0))

            def part_stats(h):
                dve.wait_ge(x_loaded[h], 16)
                tiles_of_part = part_tiles(h)
                for i in range(T // PARTS):
                    step.later(dve.bn_stats(BST[:, i, :], X[:, tiles_of_part.start + i, :]))
                moments(ALL, tiles_of_part).then_inc(var_ready, 1)

            def first_rows(k):
                dve.wait_ge(rstd_ready, k * PARTS // GROUPS + 1)
                rows_of(k, k, k, ALL, lambda i: slice(k * TG + i, k * TG + i + 1))

            def first_route(k):
                dve.wait_ge(stok_ready, k * PARTS // GROUPS + 1)
                scale_logits(k, ALL["stok"][:, tiles(k)], ROUTER[1])
                dve.wait_ge(lg_used, k + 1)
                choose(k, k)
                if k + 2 < GROUPS:
                    first_rows(k + 2)
                take_prefixes(k, ROUTER[2])
                rows_in_regions(k, k, k)

            for h in range(PARTS - 1):
                part_stats(h)
            dve.wait_ge(w_loaded, 16 * WEIGHT_LOADS)
            step(dve.tensor_copy(BT[:, 0, :], REG0))
            dve.wait_ge(pool_consts, 1)
            dve.tensor_copy(FILL[:, :, D].bitcast(U32), FROW).then_inc(fill_ready, 1)
            dve.tensor_scalar(RWS[:, :], RW[:, :], RS[:, :], float(D) ** -0.5, ALU.mult, ALU.mult).then_inc(consts_set, 1)
            first_rows(0)
            first_rows(1)
            part_stats(PARTS - 1)
            for k in range(GROUPS):
                first_route(k)
            table(0)
            ffn(0)
            weigh(0)
            for g in range(-1, 2):
                for j in range(UNITS):
                    attend(g, j)
            with dve.Fori(2, GROUPS - 1) as g:
                step.enter(g, 2, STEPS_GROUP)
                for j in range(UNITS):
                    attend(g, j)
                step.leave(GROUPS - 3)
            for g in range(GROUPS - 1, GROUPS + 2):
                for j in range(UNITS):
                    attend(g, j)
            table(1)
            ffn(1)
            weigh(1)
            dve.sem_inc(cw_ready, 1)
            combine_last()


def kernel(L0_attn_x, L0_attn_Wq, L0_attn_bq, L0_attn_Wk, L0_attn_bk, L0_attn_Wv, L0_attn_bv, L0_attn_Wo,
           L0_attn_bo, L0_ffn_router_scale, L0_ffn_router_w, L0_ffn_gating_w, L0_ffn_linear_w,
           L0_ffn_per_expert_scale):
    import numpy as np
    import concourse.bacc as bacc
    from concourse.bass_utils import run_bass_kernel_spmd

    def rows(v):
        return np.ascontiguousarray(np.broadcast_to(np.asarray(v)[None, :], (P, len(v))))

    pair_order = np.arange(D).reshape(2, NP, DH).transpose(1, 0, 2).reshape(-1)
    gates = np.asarray(L0_ffn_gating_w).transpose(3, 0, 1, 2).reshape(P, E, GW)
    linear = np.asarray(L0_ffn_linear_w).reshape(E, 2, P, D).transpose(2, 0, 1, 3).reshape(P, E, 2 * D)
    part, n_k = np.arange(P), TG * GROUPS + 1

    query_mask = (part % HALF)[:, None] // DH == np.arange(NP)[None, :]
    consts = np.concatenate([
        np.eye(P), part[:, None] < part[None, :], np.ones((P, P)), query_mask,
        np.tile(np.arange(E), (P, 1)), np.tile(np.arange(E) * REGION, (P, 1)),
        np.tile(np.arange(n_k) * P, (P, E)), np.tile(np.repeat(np.arange(SLOTS), E), (P, 1)),
        np.tile((np.arange(E)[None, :] <= np.arange(E)[:, None]).reshape(-1), (P, 1)),
        np.tile(np.arange(SLOTS), (P, 1)), part[:, None] + np.arange(T) * P,
        part[:, None] + TOPK * NSEQ * L + np.arange(FILLERS) * P], axis=1).astype(np.float32)
    arrays = dict(
        x=np.asarray(L0_attn_x).reshape(NSEQ * L, D),
        wq=np.asarray(L0_attn_Wq)[pair_order].T, bq=np.asarray(L0_attn_bq)[pair_order].reshape(P, 1),
        wk=np.asarray(L0_attn_Wk)[pair_order].T, bk=np.asarray(L0_attn_bk)[pair_order].reshape(P, 1),
        wv=np.asarray(L0_attn_Wv)[pair_order].T, bv=rows(np.asarray(L0_attn_bv)[pair_order]),
        wo=np.asarray(L0_attn_Wo).T, bo=rows(L0_attn_bo),
        rscale=np.asarray(L0_ffn_router_scale).reshape(P, 1), rw=np.asarray(L0_ffn_router_w),
        experts=np.concatenate([gates, linear], axis=2).reshape(P, E * EW),
        pes=rows(L0_ffn_per_expert_scale), consts=consts)
    arrays = {n: np.ascontiguousarray(a) for n, a in arrays.items()}
    nc = bacc.Bacc("TRN2", target_bir_lowering=False, num_devices=1)
    aps = {n: nc.dram_tensor(n, a.shape, F32, kind="ExternalInput").ap() for n, a in arrays.items()}
    out = nc.dram_tensor("out", (NSEQ * L, D), F32, kind="ExternalOutput").ap()
    macaron(nc, out=out, **aps)
    r = run_bass_kernel_spmd(nc, [arrays], core_ids=[0])
    return np.asarray(r.results[0]["out"]).reshape(NSEQ, L, D)
```
